# Optimizing a Trainium2 kernel written in Bass

```python
import numpy as np
import jax
import jax.numpy as jnp

def _softmax(x, axis=-1):
    return jax.nn.softmax(x, axis=axis)

def _gelu(x):
    return jax.nn.gelu(x, approximate=True)

def _silu(x):
    return jax.nn.silu(x)

def _sigmoid(x):
    return jax.nn.sigmoid(x)

def _layernorm(x, axis=-1, eps=1e-05):
    m = jnp.mean(x, axis=axis, keepdims=True)
    v = jnp.var(x, axis=axis, keepdims=True)
    return (x - m) / jnp.sqrt(v + eps)

def _scatter_add(tgt, idx, src, axis=0):
    return tgt.at[idx].add(src)

def _segment_sum(src, seg, n):
    return jax.ops.segment_sum(src, seg, n)
kernel_name = 'mk_xattn_seq_d2_seqx_r4_e4fad8'

def setup_inputs(seed: int=0):
    np.random.seed(seed)
    _w = jnp.asarray

    def _rec_inputs():
        import jax
        import jax.numpy as jnp
        _rk = jax.random.key(seed)
        x = -0.0001108 + 0.9999 * jax.random.normal(jax.random.fold_in(_rk, 1), (4, 512, 320), jnp.float32)
        _lenS = 512 - jax.random.randint(jax.random.fold_in(_rk, 7), (4,), 0, max(1, 512 // 4) + 1, jnp.int32)
        _lenS2 = 512 - jax.random.randint(jax.random.fold_in(_rk, 8), (4,), 0, max(1, 512 // 4) + 1, jnp.int32)
        _ctx_2048P = jax.random.normal(jax.random.fold_in(_rk, 11), (4, 16, 512), jnp.float32)
        _ctx_2048c = jax.random.dirichlet(jax.random.fold_in(_rk, 511), 0.3 * jnp.ones((16,), jnp.float32), (4, 512))
        _ctx_2048t = jnp.einsum('bsk,bkd->bsd', _ctx_2048c, _ctx_2048P)
        _ctx_2048t = _ctx_2048t * jax.lax.rsqrt(jnp.mean(jnp.square(_ctx_2048t)) + 1e-12) * 0.953939
        ctx_2048 = -0.000395056 + 1.00006 * (_ctx_2048t + 0.3 * jax.random.normal(jax.random.fold_in(_rk, 611), (4, 512, 512), jnp.float32))
        fside_S_0 = jax.random.uniform(jax.random.fold_in(_rk, 12), (512,), jnp.float32, 0.0, 0.999706)
        return (x, ctx_2048, fside_S_0)
    x, ctx_2048, fside_S_0 = _rec_inputs()

    def _L0_xattn_setup():
        import jax, jax.numpy as jnp
        import numpy as np
        NUM_HEADS = 20
        TEXT_LEN = 77
        IP_SCALE = 1.0

        def _attend(q, k, v, sm_scale):
            scores = jnp.einsum('bhsd,bhld->bhsl', q, k) * sm_scale
            probs = jax.nn.softmax(scores, axis=-1)
            return jnp.einsum('bhsl,bhld->bhsd', probs, v)

        def _split_heads(x, h):
            b, s, c = x.shape
            return x.reshape(b, s, h, c // h).transpose(0, 2, 1, 3)

        def _merge_heads(x):
            b, h, s, d = x.shape
            return x.transpose(0, 2, 1, 3).reshape(b, s, h * d)
        key = jax.random.key(seed)
        ks = jax.random.split(key, 8)
        B, S, C, CC, L = (8, 1024, 320, 512, TEXT_LEN + 4)
        sd_q = 1.0 / np.sqrt(C)
        sd_kv = 1.0 / np.sqrt(CC)
        return {'hidden_states': jax.random.normal(ks[0], (B, S, C), jnp.float32), 'encoder_hidden_states': jax.random.normal(ks[1], (B, L, CC), jnp.float32), 'Wq': jax.random.normal(ks[2], (C, C), jnp.float32) * sd_q, 'Wk': jax.random.normal(ks[3], (C, CC), jnp.float32) * sd_kv, 'Wv': jax.random.normal(ks[4], (C, CC), jnp.float32) * sd_kv, 'Wk_ip': jax.random.normal(ks[5], (C, CC), jnp.float32) * sd_kv, 'Wv_ip': jax.random.normal(ks[6], (C, CC), jnp.float32) * sd_kv, 'Wo': jax.random.normal(ks[7], (C, C), jnp.float32) * sd_q, 'bo': jnp.zeros((C,), jnp.float32)}
    _L0_xattn_all = _L0_xattn_setup()
    _L0_xattn_in = {k: v for k, v in _L0_xattn_all.items() if k in ('Wq', 'Wk', 'Wv', 'Wk_ip', 'Wv_ip', 'Wo', 'bo')}
    del _L0_xattn_all

    def _L1_xattn_setup():
        import jax, jax.numpy as jnp
        import numpy as np
        HEADS = 20
        NUM_TOKENS = 4
        IP_SCALE = 1.0
        SEM_SCALE = 0.5
        RESCALE = 1.0
        EPS = 1e-12

        def _l2norm(x, axis=-1):
            n = jnp.sqrt(jnp.sum(x * x, axis=axis, keepdims=True))
            return x / jnp.maximum(n, EPS)
        key = jax.random.key(seed)
        ks = jax.random.split(key, 10)
        B, S, C = (2, 256, 320)
        T, E = (81, 512)
        inp = {'hidden_states': jax.random.normal(ks[0], (B, S, C), jnp.float32), 'encoder_hidden_states': jax.random.normal(ks[1], (B, T, E), jnp.float32), 'spatial_mask': jax.random.uniform(ks[2], (S,), jnp.float32), 'W_q': jax.random.normal(ks[3], (C, C), jnp.float32) * C ** (-0.5), 'W_k': jax.random.normal(ks[4], (E, C), jnp.float32) * E ** (-0.5), 'W_v': jax.random.normal(ks[5], (E, C), jnp.float32) * E ** (-0.5), 'W_k_ip': jax.random.normal(ks[6], (E, C), jnp.float32) * E ** (-0.5), 'W_v_ip': jax.random.normal(ks[7], (E, C), jnp.float32) * E ** (-0.5), 'W_out': jax.random.normal(ks[8], (C, C), jnp.float32) * C ** (-0.5), 'b_out': jnp.zeros((C,), jnp.float32)}
        return inp
    _L1_xattn_all = _L1_xattn_setup()
    _L1_xattn_in = {k: v for k, v in _L1_xattn_all.items() if k in ('W_q', 'W_k', 'W_v', 'W_k_ip', 'W_v_ip', 'W_out', 'b_out')}
    del _L1_xattn_all
    return {'x': x, 'ctx_2048': ctx_2048, 'fside_S_0': fside_S_0, 'L0_xattn_Wq': _L0_xattn_in['Wq'], 'L0_xattn_Wk': _L0_xattn_in['Wk'], 'L0_xattn_Wv': _L0_xattn_in['Wv'], 'L0_xattn_Wk_ip': _L0_xattn_in['Wk_ip'], 'L0_xattn_Wv_ip': _L0_xattn_in['Wv_ip'], 'L0_xattn_Wo': _L0_xattn_in['Wo'], 'L0_xattn_bo': _L0_xattn_in['bo'], 'L1_xattn_W_q': _L1_xattn_in['W_q'], 'L1_xattn_W_k': _L1_xattn_in['W_k'], 'L1_xattn_W_v': _L1_xattn_in['W_v'], 'L1_xattn_W_k_ip': _L1_xattn_in['W_k_ip'], 'L1_xattn_W_v_ip': _L1_xattn_in['W_v_ip'], 'L1_xattn_W_out': _L1_xattn_in['W_out'], 'L1_xattn_b_out': _L1_xattn_in['b_out']}

def reference(x, ctx_2048, fside_S_0, L0_xattn_Wq, L0_xattn_Wk, L0_xattn_Wv, L0_xattn_Wk_ip, L0_xattn_Wv_ip, L0_xattn_Wo, L0_xattn_bo, L1_xattn_W_q, L1_xattn_W_k, L1_xattn_W_v, L1_xattn_W_k_ip, L1_xattn_W_v_ip, L1_xattn_W_out, L1_xattn_b_out):
    import jax
    import jax.numpy as jnp

    def _L0_xattn_ref(hidden_states, encoder_hidden_states, Wq, Wk, Wv, Wk_ip, Wv_ip, Wo, bo):
        import jax, jax.numpy as jnp
        import numpy as np
        NUM_HEADS = 20
        TEXT_LEN = 77
        IP_SCALE = 1.0

        def _attend(q, k, v, sm_scale):
            scores = jnp.einsum('bhsd,bhld->bhsl', q, k) * sm_scale
            probs = jax.nn.softmax(scores, axis=-1)
            return jnp.einsum('bhsl,bhld->bhsd', probs, v)

        def _split_heads(x, h):
            b, s, c = x.shape
            return x.reshape(b, s, h, c // h).transpose(0, 2, 1, 3)

        def _merge_heads(x):
            b, h, s, d = x.shape
            return x.transpose(0, 2, 1, 3).reshape(b, s, h * d)
        residual = hidden_states
        B, S, C = hidden_states.shape
        H = NUM_HEADS
        D = C // H
        sm_scale = 1.0 / jnp.sqrt(jnp.asarray(D, hidden_states.dtype))
        text = encoder_hidden_states[:, :TEXT_LEN, :]
        ip = encoder_hidden_states[:, TEXT_LEN:, :]
        q = _split_heads(hidden_states @ Wq.T, H)
        k = _split_heads(text @ Wk.T, H)
        v = _split_heads(text @ Wv.T, H)
        out_text = _merge_heads(_attend(q, k, v, sm_scale))
        k_ip = _split_heads(ip @ Wk_ip.T, H)
        v_ip = _split_heads(ip @ Wv_ip.T, H)
        out_ip = _merge_heads(_attend(q, k_ip, v_ip, sm_scale))
        out = out_text + IP_SCALE * out_ip
        out = out @ Wo.T + bo
        return out + residual

    def _L1_xattn_ref(hidden_states, encoder_hidden_states, spatial_mask, W_q, W_k, W_v, W_k_ip, W_v_ip, W_out, b_out):
        import jax, jax.numpy as jnp
        import numpy as np
        HEADS = 20
        NUM_TOKENS = 4
        IP_SCALE = 1.0
        SEM_SCALE = 0.5
        RESCALE = 1.0
        EPS = 1e-12

        def _l2norm(x, axis=-1):
            n = jnp.sqrt(jnp.sum(x * x, axis=axis, keepdims=True))
            return x / jnp.maximum(n, EPS)
        B, S, C = hidden_states.shape
        H = HEADS
        Dh = C // H
        attn_scale = Dh ** (-0.5)
        residual = hidden_states
        text_ehs = encoder_hidden_states[:, :-NUM_TOKENS]
        ip_ehs = encoder_hidden_states[:, -NUM_TOKENS:]

        def heads(x):
            return x.reshape(B, -1, H, Dh).transpose(0, 2, 1, 3)
        q = heads(hidden_states @ W_q)
        k_t = heads(text_ehs @ W_k)
        v_t = heads(text_ehs @ W_v)
        scores_t = jnp.einsum('bhsd,bhtd->bhst', q, k_t) * attn_scale
        probs_t = jax.nn.softmax(scores_t, axis=-1)
        text_out = jnp.einsum('bhst,bhtd->bhsd', probs_t, v_t)
        text_out = text_out.transpose(0, 2, 1, 3).reshape(B, S, C)
        k_ip = heads(ip_ehs @ W_k_ip)
        v_ip = heads(ip_ehs @ W_v_ip)
        attn_scores = jnp.einsum('bhsd,bhnd->bhsn', q, k_ip) * attn_scale
        qsem = jnp.einsum('bhst,bte->bhse', probs_t, text_ehs)
        qsem = _l2norm(qsem)
        ip_n = _l2norm(ip_ehs)
        sem = jnp.einsum('bhse,bne->bhsn', qsem, ip_n)
        sem = jax.lax.stop_gradient(sem)
        fused = attn_scores + SEM_SCALE * sem
        probs_ip = jax.nn.softmax(fused, axis=-1)
        probs_ip = probs_ip * spatial_mask[None, None, :, None]
        ip_out = jnp.einsum('bhsn,bhnd->bhsd', probs_ip, v_ip)
        ip_out = ip_out.transpose(0, 2, 1, 3).reshape(B, S, C)
        out = text_out + IP_SCALE * ip_out
        out = out @ W_out + b_out
        out = out + residual
        return out / RESCALE
    x = _L0_xattn_ref(x, ctx_2048, L0_xattn_Wq, L0_xattn_Wk, L0_xattn_Wv, L0_xattn_Wk_ip, L0_xattn_Wv_ip, L0_xattn_Wo, L0_xattn_bo)
    x = _L1_xattn_ref(x, ctx_2048, fside_S_0, L1_xattn_W_q, L1_xattn_W_k, L1_xattn_W_v, L1_xattn_W_k_ip, L1_xattn_W_v_ip, L1_xattn_W_out, L1_xattn_b_out)
    return x

_drawn_inputs = setup_inputs


def setup_inputs(seed=0):
    import zlib

    import numpy as np

    out = dict(_drawn_inputs(seed))
    spreads = {'L0_xattn_bo': (0.0, 0.1), 'L1_xattn_b_out': (0.0, 0.1)}
    factors = {}
    for name, (base, spread) in spreads.items():
        noise = np.random.default_rng([zlib.crc32(name.encode()), seed]).standard_normal(out[name].shape)
        drawn = base * np.exp(spread * noise) if base else spread * noise
        out[name] = jnp.asarray(drawn.astype(out[name].dtype))
    for name, factor in factors.items():
        out[name] = (out[name] * factor).astype(out[name].dtype)
    return out
```

```python
from contextlib import ExitStack

import concourse.bass as bass
from concourse import mybir

ACT = mybir.ActivationFunctionType
ALU = mybir.AluOpType
AX = mybir.AxisListType
F32 = mybir.dt.float32
F32R = mybir.dt.float32r

P = 128
BATCH, S, C, E, T = 4, 512, 320, 512, 512
HEADS, D = 20, 16
PAIRS = HEADS // 2
TEXT0 = 77
IPN = 4
TEXT1 = T - IPN
SCALE = float(D) ** -0.5
SEM_SCALE = 0.5
EPS = 1e-12
SC = S // P
TB = T // P
EB = E // P
CB = [P, P, C - 2 * P]
CBN = len(CB)

PART = D
SCORE_ROWS = 3 * PART
SHIFT_ROW = 64
SHIFT_ROWS = 33
ALL_ROWS = SHIFT_ROW + SHIFT_ROWS
SLOT_LOADS = 6 * 16

V0W = 2 * (D + 1)
GA = T - P
GW = GA + D
GN = TEXT1 - P
OUT1 = 24
A1, V1, NA, NB = 0, IPN, IPN + D, IPN + D + 1
SZW = 8

JOBS = (
    [("k0", m, "D") for m in range(CBN)]
    + [("q0", m, "D") for m in range(CBN)]
    + [("k1", m, "D") for m in range(CBN)]
    + [("v0t", 0, "A")]
    + [("v0i", t, "A") for t in range(TB)]
    + [("g", i, "A") for i in range(TB)]
    + [("v1", t, "D") for t in range(TB)]
    + [("ipn", 0, "D"), ("vip", 0, "D")]
    + [("vrep", n, "D") for n in range(IPN)]
    + [("tr0", m, "A") for m in range(CBN)]
    + [("x1", m, "D") for m in range(CBN)]
    + [("q1", m, "D") for m in range(CBN)]
    + [("tr1", m, "A") for m in range(CBN)]
    + [("y", m, "D") for m in range(CBN)]
)
JOB = {(name, m): k for k, (name, m, _) in enumerate(JOBS)}
FREED_BY = [e for _, _, e in JOBS]
PER_B = {e: FREED_BY.count(e) for e in "AD"}
RING = 4
WEIGHTS = 16 * (8 + 8 + 2 * CBN + 1)
CREDIT = 8


def build(nc, xT, ctxT, mask, wq0, wk0, wv0, wki0, wvi0, wo0, bo0, wq1, wk1, wv1, wki1, wvi1, wo1, bo1, outT):
    with ExitStack() as ctx:
        def sb(name, shape, dt=F32):
            return ctx.enter_context(nc.sbuf_tensor(name, shape, dt))

        def sem(name):
            return ctx.enter_context(nc.semaphore(name))

        scratch = {n: nc.dram_tensor(f"parts_{n}", [2, HEADS, D, S], F32, kind="Internal").ap()
                   for n in ("k0", "q0", "k1", "q1")}

        w_small = {n: sb(f"w_{n}", [P, CBN, C]) for n in ("q0", "o0", "q1", "o1")}
        w_big = {n: sb(f"w_{n}", [P, EB, C]) for n in ("k0", "v0", "ki0", "vi0", "k1", "v1", "ki1", "vi1")}
        bias_o = [sb(f"bias_o{l}", [P, CBN]) for l in range(2)]
        mask_sb = sb("mask_sb", [P, SC])
        ctx_sb = sb("ctx_sb", [P, EB, T])
        x_sb = sb("x_sb", [P, CBN, S])
        x1_sb = sb("x1_sb", [P, CBN, S])
        ident = sb("ident", [P, P])
        ident_r = sb("ident_r", [P, P], F32R)
        ones = sb("ones", [P, P])
        pick = sb("pick", [IPN, IPN, P])
        ip_rows = sb("ip_rows", [P, 1])
        v0_sb = sb("v0_sb", [P, TB, HEADS, V0W])
        v1_sb = sb("v1_sb", [P, TB, C])
        gram00 = sb("gram00", [P, P])
        gram = [sb(f"gram{p}", [P, TB, GW]) for p in range(2)]
        ip_sq = sb("ip_sq", [P, EB, IPN])
        vip = sb("vip", [IPN, C])
        vip_rep = sb("vip_rep", [P, IPN, C])
        q_slot = [sb(f"q_slot{p}", [ALL_ROWS, S], F32R) for p in range(2)]
        k_slot = [[sb(f"k_slot{l}{p}", [ALL_ROWS, T], F32R) for p in range(2)] for l in range(2)]
        row_max = [[sb(f"row_max{l}{p}", [P, SC, SHIFT_ROWS], F32R) for p in range(2)] for l in range(2)]
        probsT = [sb(f"probsT{p}", [P, TB, S]) for p in range(2)]
        probs = [sb(f"probs{p}", [P, SC, S]) for p in range(2)]
        parts_q = sb("parts_q", [P, 2, CBN, S])
        exp_bias = [sb(f"exp_bias{p}", [P, SC]) for p in range(2)]
        sz = [sb(f"sz{p}", [P, SC, SZW]) for p in range(2)]
        head_out = [sb(f"head_out{p}", [P, SC, OUT1]) for p in range(2)]
        out_all = sb("out_all", [P, HEADS * SC * V0W])
        o0_all = out_all[:, :].rearrange("p (h c w) -> p h c w", h=HEADS, c=SC)
        o1_all = out_all[:, 0:HEADS * SC * OUT1].rearrange("p (h c w) -> p h c w", h=HEADS, c=SC)
        sz_all = sb("sz_all", [P, HEADS, SC, SZW])
        dump = sb("dump", [P, 64])
        heads_out = sb("heads_out", [P, SC, C])
        heads_outT = sb("heads_outT", [P, CBN, S])
        nd = HEADS * SC
        stat = sb("stat", [P, nd, 8])
        root = sb("root", [P, nd + IPN])
        ip_norm2 = sb("ip_norm2", [P, IPN])
        rip = sb("rip", [P, IPN])
        fused = sb("fused", [P, nd, IPN])
        wide = [probs[i][:, :, :].rearrange("p c s -> p (c s)")[:, 0:nd * D].rearrange("p (n d) -> p n d", d=D)
                for i in range(2)]
        parts = {"k0": [probsT[0][:, 0:CBN, :], probsT[1][:, 0:CBN, :]],
                 "k1": [probs[0][:, 0:CBN, :], probs[1][:, 0:CBN, :]],
                 "q0": [parts_q[:, 0, :, :], parts_q[:, 1, :, :]],
                 "q1": [parts_q[:, 0, :, :], parts_q[:, 1, :, :]]}

        y_sb = parts_q[:, 1, :, :]

        ps_s = ctx.enter_context(nc.psum_tensor("ps_s", [P, 2, 512], F32))
        ps_t = ctx.enter_context(nc.psum_tensor("ps_t", [P, 2, 512], F32))
        ps_w = [ctx.enter_context(nc.psum_tensor(f"ps_w{i}", [P, 512], F32)) for i in range(2)]
        ps_b = ctx.enter_context(nc.psum_tensor("ps_b", [P, 512], F32))
        ps_m = ctx.enter_context(nc.psum_tensor("ps_m", [P, 512], F32))
        ring = [ps_s[:, 0, :], ps_s[:, 1, :], ps_t[:, 0, :], ps_t[:, 1, :]]

        weights_in = sem("weights_in")
        filled, built = sem("filled"), sem("built")
        ident_r_in = sem("ident_r_in")
        dve_consts_in = sem("dve_consts_in")
        ctx_in, x_in = sem("ctx_in"), sem("x_in")
        job_done = sem("job_done")
        freed = {"A": sem("freed_by_act"), "D": sem("freed_by_dve")}
        high_in = sem("high_in")
        ip_sq_in = sem("ip_sq_in")
        gram_copied = sem("gram_copied")
        stored = {n: sem(f"stored_{n}") for n in scratch}
        y_out = sem("y_out")
        passed = sem("passed")
        heads_ready = sem("heads_ready")
        chain = sem("chain")
        ask_root, root_in = sem("ask_root"), sem("root_in")
        ask_exp, exp_in = sem("ask_exp"), sem("exp_in")
        slots_in = [[sem(f"slots_in{l}{p}") for p in range(2)] for l in range(2)]
        s_half = [sem(f"s_half{l}") for l in range(2)]
        max_half = [sem(f"max_half{l}") for l in range(2)]
        maxT_done = [sem(f"maxT_done{l}") for l in range(2)]
        shift_in = [sem(f"shift_in{l}") for l in range(2)]
        st_half = [sem(f"st_half{l}") for l in range(2)]
        pt_half = [sem(f"pt_half{l}") for l in range(2)]
        o_done = sem("o_done")
        o_moved = sem("o_moved")
        bias_in = sem("bias_in")
        p_chunk = sem("p_chunk")
        v_in = sem("v_in")
        b_done, w_done = sem("b_done"), sem("w_done")
        zb_done, z_done = sem("zb_done"), sem("z_done")
        sz_moved, out_moved = sem("sz_moved"), sem("out_moved")

        def jobs_before(engine, k):
            return sum(1 for e in FREED_BY[:k] if e == engine)

        def wait_freed(eng, b, name, m):
            k = JOB[name, m]
            e = FREED_BY[k]
            eng.wait_ge(freed[e], PER_B[e] * b + CREDIT + jobs_before(e, k) + 1)

        def wait_job(eng, b, name, m):
            eng.wait_ge(job_done, len(JOBS) * b + JOB[name, m] + 1)

        def bank(name, m):
            return ring[JOB[name, m] % RING]

        def run_heads(eng, step, b):
            step(b, -2, 0, False, False, True)
            step(b, -1, 1, False, True, True)
            with eng.Fori(0, PAIRS - 1) as pair:
                step(b, 2 * pair, 0, True, True, True)
                step(b, 2 * pair + 1, 1, True, True, True)
            step(b, HEADS - 2, 0, True, True, False)
            step(b, HEADS - 1, 1, True, False, False)

        block = ctx.enter_context(nc.Block())

        @block.sync
        def _(sp):
            for n, src in (("k0", wk0), ("ki0", wki0), ("v0", wv0), ("vi0", wvi0),
                           ("k1", wk1), ("ki1", wki1), ("v1", wv1), ("vi1", wvi1)):
                sp.dma_start(w_big[n][:, :, :], src.rearrange("(k p) n -> p k n", p=P)).then_inc(weights_in, 16)
            for n, src in (("q0", wq0), ("o0", wo0), ("q1", wq1), ("o1", wo1)):
                sp.dma_start(w_small[n][:, 0:2, :], src[0:2 * P, :].rearrange("(k p) n -> p k n", p=P)).then_inc(weights_in, 16)
                sp.dma_start(w_small[n][0:CB[2], 2, :], src[2 * P:C, :]).then_inc(weights_in, 16)
            for l, src in ((0, bo0), (1, bo1)):
                for m in range(CBN):
                    sp.dma_start(bias_o[l][0:CB[m], m:m + 1], src[m * P:m * P + CB[m], :]).then_inc(weights_in, 16)
            sp.dma_start(mask_sb[:, :], mask).then_inc(weights_in, 16)

            def store(b, name):
                for part in range(2):
                    dst = scratch[name][part, :, :, :].rearrange("h d s -> (h d) s")
                    sp.dma_start(dst[0:2 * P, :].rearrange("(k p) s -> p k s", p=P),
                                 parts[name][part][:, 0:2, :]).then_inc(stored[name], 16)
                    sp.dma_start(dst[2 * P:C, :], parts[name][part][0:CB[2], 2, :]).then_inc(stored[name], 16)

            def load_slots(b, l, n, par):
                qs, ks = scratch[f"q{l}"], scratch[f"k{l}"]
                sp.wait_ge(pt_half[l], 2 * (HEADS * b + n - 1) + CREDIT)
                for i, (qp, kp) in enumerate(((0, 0), (0, 1), (1, 0))):
                    rows = slice(PART * i, PART * i + PART)
                    sp.dma_start(q_slot[par][rows, :].bitcast(F32), qs[qp, n, :, :]).then_inc(slots_in[l][par], 16)
                    sp.dma_start(k_slot[l][par][rows, :].bitcast(F32), ks[kp, n, :, :]).then_inc(slots_in[l][par], 16)

            def load_all(b, l):
                with sp.Fori(0, PAIRS) as pair:
                    load_slots(b, l, 2 * pair, 0)
                    load_slots(b, l, 2 * pair + 1, 1)

            with sp.Fori(0, BATCH) as b:
                sp.wait_ge(freed["D"], PER_B["D"] * b + CREDIT)
                sp.dma_start(ctx_sb[:, :, :], ctxT[b, :, :].rearrange("(k p) t -> p k t", p=P)).then_inc(ctx_in, 16)
                sp.dma_start(x_sb[:, 0:2, :], xT[b, 0:2 * P, :].rearrange("(k p) s -> p k s", p=P)).then_inc(x_in, 16)
                sp.dma_start(x_sb[0:CB[2], 2, :], xT[b, 2 * P:C, :]).then_inc(x_in, 16)
                for name in ("k0", "q0", "k1"):
                    wait_freed(sp, b, name, CBN - 1)
                    store(b, name)
                for name in ("k0", "q0", "k1"):
                    sp.wait_ge(stored[name], 64 * (b + 1))
                sp.sem_inc(passed, 1)
                load_all(b, 0)
                wait_freed(sp, b, "q1", CBN - 1)
                store(b, "q1")
                sp.wait_ge(stored["q1"], 64 * (b + 1))
                sp.sem_inc(passed, 1)
                load_all(b, 1)

        @block.gpsimd
        def _(pool):
            nc.gpsimd.memset(ident[:, :], 0.0).then_inc(filled, 1)
            nc.gpsimd.memset(pick[:, :, :], 0.0).then_inc(filled, 1)
            nc.gpsimd.memset(ones[:, :], 1.0).then_inc(filled, 1)
            nc.gpsimd.memset(out_all[:, 0:1], 0.0).then_inc(out_moved, CREDIT)
            pool.wait_ge(filled, 3)
            nc.gpsimd.affine_select(out=ident[:, :], in_=ident[:, :], compare_op=ALU.not_equal, fill=1.0, base=0,
                                    pattern=[[-1, P]], channel_multiplier=1).then_inc(built, 1)
            nc.gpsimd.affine_select(out=pick[:, :, :], in_=pick[:, :, :], compare_op=ALU.not_equal, fill=1.0, base=0,
                                    pattern=[[-1, IPN], [0, P]], channel_multiplier=1).then_inc(built, 1)

            def step(b, n, par, use, transposed, scores):
                g = HEADS * b + n
                if scores:
                    for half in range(2):
                        pool.wait_ge(max_half[1], 2 * (g + 2) + half + 1 + CREDIT)
                        pool.sem_inc(passed, 1)
                        nc.gpsimd.tensor_scalar_mul(exp_bias[par][:, 2 * half:2 * half + 2],
                                                    row_max[1][par][:, 2 * half:2 * half + 2, 0].bitcast(F32), -SCALE)\
                            .then_inc(bias_in, 1)
                if use:
                    pool.wait_ge(z_done, SC * (g + 1) + CREDIT)
                    pool.sem_inc(passed, 1)
                    nc.gpsimd.tensor_copy(o1_all[:, n, :, 0:OUT1 - 2], head_out[par][:, :, 0:OUT1 - 2]).then_inc(out_moved, 1)
                if scores:
                    nc.gpsimd.tensor_copy(gram[par][:, :, GA:GW], v1_sb[:, :, :].rearrange("p t (h d) -> p t h d", d=D)[:, :, n + 2, :])\
                        .then_inc(v_in, 1)
                    pool.wait_ge(p_chunk, SC * (g + 3) + CREDIT)
                    pool.sem_inc(passed, 1)
                    nc.gpsimd.tensor_copy(sz_all[:, n + 2, :, 0:IPN + 1], sz[par][:, :, 0:IPN + 1]).then_inc(sz_moved, 1)

            with pool.Fori(0, BATCH) as b:
                wait_freed(pool, b, "g", TB - 1)
                pool.sem_inc(passed, 1)
                for i in range(TB):
                    lo = P * max(i, 1) - P
                    last = nc.gpsimd.tensor_copy(gram[1][:, i, lo:GA], gram[0][:, i, lo:GA])
                last.then_inc(gram_copied, 1)
                wait_freed(pool, b, "v1", TB - 1)
                pool.sem_inc(passed, 1)
                run_heads(pool, step, b)

        @block.scalar
        def _(act):
            act.wait_ge(built, 2)
            nc.scalar.activation(ident_r[:, :], ident[:, :], ACT.Copy).then_inc(ident_r_in, 1)
            for i, s in enumerate((freed["A"], pt_half[0], pt_half[1], o_moved, p_chunk)):
                nc.scalar.activation(dump[:, i:i + 1], ident[:, 0:1], ACT.Copy).then_inc(s, CREDIT)
            act.wait_ge(dve_consts_in, 1)

            def high(b, name, m):
                wait_job(act, b, name, m)
                nc.scalar.activation(parts[name][0][0:CB[m], m, :].bitcast(F32R), bank(name, m)[0:CB[m], :],
                                     ACT.Copy).then_inc(high_in, 1)

            def shift(b, l, n, par):
                act.wait_ge(maxT_done[l], HEADS * b + n + 2)
                nc.scalar.activation(q_slot[1 - par][SHIFT_ROW:ALL_ROWS, :], ps_m[0:SHIFT_ROWS, :], ACT.Copy)\
                    .then_inc(shift_in[l], 1)

            def expT(b, l, n, par):
                g = HEADS * b + n
                for half in range(2):
                    act.wait_ge(st_half[l], 2 * (g + 1) + half + 1)
                    nc.scalar.activation(probsT[1 - par][:, 2 * half:2 * half + 2, :], ps_t[:, :, :], ACT.Exp,
                                         scale=SCALE).then_inc(pt_half[l], 1)

            def step0(b, n, par, use, transposed, scores):
                if transposed:
                    shift(b, 0, n, par)
                    expT(b, 0, n, par)
                if use:
                    act.wait_ge(o_done, HEADS * b + n + 1)
                    nc.scalar.activation(o0_all[:, n, :, :], ps_w[par][:, 0:SC * V0W].rearrange("p (c w) -> p c w", c=SC),
                                         ACT.Copy).then_inc(o_moved, 1)

            def step1(b, n, par, use, transposed, scores):
                g = HEADS * b + n
                if transposed:
                    shift(b, 1, n, par)
                    expT(b, 1, n, par)
                if scores:
                    for c in range(SC):
                        if c % 2 == 0:
                            act.wait_ge(bias_in, 2 * (g + 2) + c // 2 + 1)
                        act.wait_ge(z_done, SC * g + c + 1 + CREDIT) if use else None
                        nc.scalar.activation(probs[par][:, c, 0:TEXT1], ps_s[:, c % 2, 0:TEXT1], ACT.Exp,
                                             bias=exp_bias[par][:, c:c + 1], scale=SCALE,
                                             accum_out=sz[par][:, c, IPN:IPN + 1]).then_inc(p_chunk, 1)

            with act.Fori(0, BATCH) as b:
                for name in ("k0", "q0", "k1"):
                    for m in range(CBN):
                        high(b, name, m)
                wait_job(act, b, "v0t", 0)
                nc.scalar.activation(v0_sb[0:TEXT0, 0, :, 0:D],
                                     bank("v0t", 0)[0:TEXT0, 0:C].rearrange("p (h d) -> p h d", d=D),
                                     ACT.Copy).then_inc(freed["A"], 1)
                for t in range(TB):
                    wait_job(act, b, "v0i", t)
                    nc.scalar.activation(v0_sb[:, t, :, D + 1:2 * D + 1],
                                         bank("v0i", t)[:, 0:C].rearrange("p (h d) -> p h d", d=D),
                                         ACT.Copy, scale=ip_rows[:, :] if t == 0 else 1.0).then_inc(freed["A"], 1)
                for i in range(TB):
                    wait_job(act, b, "g", i)
                    src = bank("g", i)
                    diag = P if i < TB - 1 else P - IPN
                    dst = gram00[:, :] if i == 0 else gram[0][:, i, P * (i - 1):P * (i - 1) + diag]
                    nc.scalar.activation(dst, src[:, 0:diag], ACT.Copy)
                    nc.scalar.activation(gram[0][:, i, P * i - P + diag:GA], src[:, diag:T - P * i], ACT.Copy, scale=2.0)\
                        .then_inc(freed["A"], 1)
                run_heads(act, step0, b)
                for m in range(CBN):
                    wait_job(act, b, "tr0", m)
                    nc.scalar.activation(heads_outT[0:CB[m], m, :], bank("tr0", m)[0:CB[m], :], ACT.Copy).then_inc(freed["A"], 1)
                for m in range(CBN):
                    high(b, "q1", m)
                run_heads(act, step1, b)
                act.wait_ge(ask_root, b + 1)
                nc.scalar.activation(root[:, :], root[:, :], ACT.Sqrt).then_inc(root_in, 1)
                act.wait_ge(ask_exp, b + 1)
                nc.scalar.activation(fused[:, :, :], fused[:, :, :], ACT.Exp).then_inc(exp_in, 1)
                for m in range(CBN):
                    wait_job(act, b, "tr1", m)
                    nc.scalar.activation(heads_outT[0:CB[m], m, :], bank("tr1", m)[0:CB[m], :], ACT.Copy).then_inc(freed["A"], 1)
                for m in range(CBN):
                    wait_freed(act, b, "y", m)
                    act.dma_start(outT[b, m * P:m * P + CB[m], :], y_sb[0:CB[m], m, :]).then_inc(y_out, 16)
            act.wait_ge(y_out, 16 * CBN * BATCH + 16)

        @block.vector
        def _(dve):
            for i, s in enumerate((freed["D"], max_half[0], max_half[1], z_done, zb_done)):
                nc.vector.memset(stat[:, i, 0:1], 0.0).then_inc(s, CREDIT)
            nc.vector.memset(stat[:, 5, 0:1], 0.0).then_inc(y_out, 16)
            zero = [t[:, :] for t in q_slot + k_slot[0] + k_slot[1]] + [t[:, :, :] for t in row_max[0] + row_max[1]]
            for t in zero:
                nc.vector.memset(t.bitcast(F32), 0.0)
            nc.vector.memset(v0_sb[:, :, :, :], 0.0)
            nc.vector.memset(ip_rows[:, :], 1.0)
            nc.vector.memset(dump[:, 8:9], 0.0).then_inc(chain, 1)
            dve.wait_ge(chain, 1)
            for p in range(2):
                nc.vector.memset(k_slot[0][p][SHIFT_ROW:SHIFT_ROW + 1, 0:TEXT0].bitcast(F32), -1.0)
                nc.vector.memset(k_slot[0][p][ALL_ROWS - 1:ALL_ROWS, TEXT0:T].bitcast(F32), -1.0)
                nc.vector.memset(k_slot[1][p][SHIFT_ROW:SHIFT_ROW + 1, :].bitcast(F32), -1.0)
            nc.vector.memset(ip_rows[0:TEXT0, :], 0.0)
            nc.vector.memset(v0_sb[:, :, :, 2 * D + 1:V0W], 1.0)
            nc.vector.memset(v0_sb[0:TEXT0, 0, :, D:D + 1], 1.0).then_inc(chain, 1)
            dve.wait_ge(chain, 2)
            nc.vector.memset(v0_sb[0:TEXT0, 0, :, 2 * D + 1:V0W], 0.0).then_inc(dve_consts_in, 1)
            CHAIN0 = 2
            links = [0]
            CHAIN_B = 26

            def link(b, ins):
                links[0] += 1
                ins.then_inc(chain, 1)
                dve.wait_ge(chain, CHAIN_B * b + links[0] + CHAIN0)

            def low(b, name, m):
                wait_job(dve, b, name, m)
                k = ["k0", "q0", "k1", "q1"].index(name) * CBN + m
                dve.wait_ge(high_in, 4 * CBN * b + k + 1)
                nc.vector.tensor_tensor(parts[name][1][0:CB[m], m, :], bank(name, m)[0:CB[m], :],
                                        parts[name][0][0:CB[m], m, :], ALU.subtract).then_inc(freed["D"], 1)

            def step0(b, n, par, use, transposed, scores):
                if scores:
                    for half in range(2):
                        cs = slice(2 * half, 2 * half + 2)
                        dve.wait_ge(s_half[0], 2 * (HEADS * b + n + 2) + half + 1)
                        nc.vector.tensor_reduce(out=row_max[0][par][:, cs, 0:1], in_=ps_s[:, :, 0:TEXT0], axis=AX.X, op=ALU.max)
                        nc.vector.tensor_reduce(out=row_max[0][par][:, cs, SHIFT_ROWS - 1:SHIFT_ROWS], in_=ps_s[:, :, TEXT0:T],
                                                axis=AX.X, op=ALU.max).then_inc(max_half[0], 1)

            def step1(b, n, par, use, transposed, scores):
                g = HEADS * b + n

                def maxima(half):
                    cs = slice(2 * half, 2 * half + 2)
                    if half == 0:
                        dve.wait_ge(sz_moved, g + 1) if use else None
                    dve.wait_ge(s_half[1], 2 * (g + 2) + half + 1)
                    nc.vector.tensor_copy(sz[par][:, cs, 0:IPN], ps_s[:, :, TEXT1:T])
                    nc.vector.tensor_reduce(out=row_max[1][par][:, cs, 0:1], in_=ps_s[:, :, 0:TEXT1], axis=AX.X,
                                            op=ALU.max).then_inc(max_half[1], 1)

                if not use:
                    if scores:
                        maxima(0)
                        maxima(1)
                    return
                out = head_out[par]
                dve.wait_ge(b_done, g + 1)
                dve.wait_ge(p_chunk, SC * (g + 1) + CREDIT)
                dve.wait_ge(out_moved, g - 1 + CREDIT)
                for c in range(SC):
                    last = nc.vector.tensor_tensor_reduce(out=probs[par][:, c, 0:P], in0=ps_b[:, P * c:P * c + P], in1=probs[par][:, c, 0:P],
                                                          scale=1.0, scalar=0.0, op0=ALU.mult, op1=ALU.add,
                                                          accum_out=out[:, c, NB:NB + 1])
                last.then_inc(zb_done, 1)
                for c in range(SC):
                    dve.wait_ge(w_done, SC * g + c + 1)
                    nc.vector.tensor_copy(out[:, c, 0:IPN + D], ps_w[c % 2][:, GN:GW])
                    nc.vector.tensor_tensor_reduce(out=probs[par][:, c, P:TEXT1], in0=ps_w[c % 2][:, 0:GN], in1=probs[par][:, c, P:TEXT1],
                                                   scale=1.0, scalar=0.0, op0=ALU.mult, op1=ALU.add,
                                                   accum_out=out[:, c, NA:NA + 1]).then_inc(z_done, 1)
                    if scores and c in (1, 2):
                        maxima(c - 1)

            with dve.Fori(0, BATCH) as b:
                links[0] = 0
                dve.wait_ge(y_out, 16 * CBN * b + 16)
                for name in ("k0", "q0", "k1"):
                    for m in range(CBN):
                        low(b, name, m)
                dve.wait_ge(ctx_in, 16 * b + 16)
                nc.vector.tensor_tensor(ip_sq[:, :, :], ctx_sb[:, :, TEXT1:T], ctx_sb[:, :, TEXT1:T], ALU.mult)\
                    .then_inc(ip_sq_in, 1)
                for t in range(TB):
                    wait_job(dve, b, "v1", t)
                    nc.vector.tensor_copy(v1_sb[:, t, :], bank("v1", t)[:, 0:C]).then_inc(freed["D"], 1)
                wait_job(dve, b, "ipn", 0)
                nc.vector.tensor_copy(ip_norm2[:, :], bank("ipn", 0)[:, 0:IPN]).then_inc(freed["D"], 1)
                wait_job(dve, b, "vip", 0)
                nc.vector.tensor_copy(vip[:, :], bank("vip", 0)[0:IPN, 0:C]).then_inc(freed["D"], 1)
                for i in range(IPN):
                    wait_job(dve, b, "vrep", i)
                    nc.vector.tensor_copy(vip_rep[:, i, :], bank("vrep", i)[:, 0:C]).then_inc(freed["D"], 1)

                run_heads(dve, step0, b)
                dve.wait_ge(o_moved, HEADS * (b + 1) + CREDIT)
                o0 = out_all[:, :].rearrange("p (n w) -> p n w", w=V0W)
                zr = stat[:, :, 0:2]
                link(b, nc.vector.reciprocal(zr, o0.rearrange("p n (a w) -> p n a w", a=2)[:, :, :, D]))
                nc.vector.tensor_tensor(wide[0], o0[:, :, 0:D], stat[:, :, 0:1].to_broadcast([P, nd, D]), ALU.mult)
                link(b, nc.vector.tensor_tensor(wide[1], o0[:, :, D + 1:2 * D + 1], stat[:, :, 1:2].to_broadcast([P, nd, D]), ALU.mult))
                by_head = heads_out[:, :, :].rearrange("p c (h d) -> p h c d", d=D)
                w4 = [w.rearrange("p (h c) d -> p h c d", c=SC) for w in wide]
                nc.vector.tensor_tensor(by_head, w4[0], w4[1], ALU.add).then_inc(heads_ready, 1)
                for m in range(CBN):
                    wait_job(dve, b, "x1", m)
                    nc.vector.scalar_tensor_tensor(out=x1_sb[0:CB[m], m, :], in0=bank("x1", m)[0:CB[m], :],
                                                   scalar=bias_o[0][0:CB[m], m:m + 1], in1=x_sb[0:CB[m], m, :],
                                                   op0=ALU.add, op1=ALU.add).then_inc(freed["D"], 1)
                for m in range(CBN):
                    low(b, "q1", m)

                run_heads(dve, step1, b)
                dve.wait_ge(out_moved, HEADS * (b + 1) + CREDIT)
                dve.wait_ge(sz_moved, HEADS * (b + 1))
                o1 = out_all[:, 0:nd * OUT1].rearrange("p (n w) -> p n w", w=OUT1)
                szf = sz_all[:, :, :, :].rearrange("p h c w -> p (h c) w")
                rz, n2, rn = stat[:, :, 2:3], stat[:, :, 3:4], stat[:, :, 4:5]
                top, tot = stat[:, :, 5:6], stat[:, :, 6:7]
                link(b, nc.vector.reciprocal(rz, szf[:, :, IPN:IPN + 1]))
                link(b, nc.vector.tensor_tensor(n2, o1[:, :, NA:NA + 1], o1[:, :, NB:NB + 1], ALU.add))
                link(b, nc.vector.tensor_tensor(n2, n2, rz, ALU.mult))
                link(b, nc.vector.tensor_tensor(n2, n2, rz, ALU.mult))
                nc.vector.tensor_scalar_max(root[:, 0:nd], stat[:, :, 3], EPS * EPS)
                nc.vector.tensor_scalar_max(root[:, nd:nd + IPN], ip_norm2[:, :], EPS * EPS).then_inc(ask_root, 1)
                dve.wait_ge(root_in, b + 1)
                nc.vector.reciprocal(rip[:, :], root[:, nd:nd + IPN])
                link(b, nc.vector.reciprocal(stat[:, :, 4], root[:, 0:nd]))
                link(b, nc.vector.tensor_tensor(rn, rn, rz, ALU.mult))
                link(b, nc.vector.tensor_tensor(fused[:, :, :], o1[:, :, A1:A1 + IPN], rn.to_broadcast([P, nd, IPN]), ALU.mult))
                for i in range(IPN):
                    last = nc.vector.tensor_scalar(fused[:, :, i], fused[:, :, i], rip[:, i:i + 1], SEM_SCALE / 2, ALU.mult, ALU.mult)
                link(b, last)
                link(b, nc.vector.scalar_tensor_tensor(out=fused[:, :, :], in0=szf[:, :, 0:IPN], scalar=SCALE, in1=fused[:, :, :],
                                                       op0=ALU.mult, op1=ALU.add))
                link(b, nc.vector.tensor_reduce(out=top, in_=fused[:, :, :], axis=AX.X, op=ALU.max))
                nc.vector.tensor_tensor(fused[:, :, :], fused[:, :, :], top.to_broadcast([P, nd, IPN]), ALU.subtract)\
                    .then_inc(ask_exp, 1)
                nc.vector.tensor_tensor(wide[0], o1[:, :, V1:V1 + D], rz.to_broadcast([P, nd, D]), ALU.mult)
                dve.wait_ge(exp_in, b + 1)
                link(b, nc.vector.tensor_reduce(out=tot, in_=fused[:, :, :], axis=AX.X, op=ALU.add))
                link(b, nc.vector.reciprocal(tot, tot))
                tot3 = stat[:, :, 6].rearrange("p (h c) -> p h c", c=SC)
                mask3 = mask_sb[:, :].unsqueeze(1).to_broadcast([P, HEADS, SC])
                link(b, nc.vector.tensor_tensor(tot3, tot3, mask3, ALU.mult))
                link(b, nc.vector.tensor_tensor(fused[:, :, :], fused[:, :, :], tot.to_broadcast([P, nd, IPN]), ALU.mult))
                f4 = fused[:, :, :].rearrange("p (h c) i -> p h c i", c=SC)
                vr = vip_rep[:, :, :].rearrange("p i (h d) -> p i h d", d=D)
                for i in range(IPN):
                    for c in range(SC):
                        last = nc.vector.tensor_tensor(w4[1][:, :, c, :], f4[:, :, c, i:i + 1].to_broadcast([P, HEADS, D]),
                                                       vr[:, i, :, :], ALU.mult)
                    link(b, last)
                    if i < IPN - 1:
                        link(b, nc.vector.tensor_tensor(wide[0], wide[0], wide[1], ALU.add))
                nc.vector.tensor_tensor(by_head, w4[0], w4[1], ALU.add).then_inc(heads_ready, 1)
                for m in range(CBN):
                    wait_job(dve, b, "y", m)
                    nc.vector.scalar_tensor_tensor(out=y_sb[0:CB[m], m, :], in0=bank("y", m)[0:CB[m], :],
                                                   scalar=bias_o[1][0:CB[m], m:m + 1], in1=x1_sb[0:CB[m], m, :],
                                                   op0=ALU.add, op1=ALU.add).then_inc(freed["D"], 1)
                assert links[0] <= CHAIN_B, links[0]
                while links[0] < CHAIN_B:
                    link(b, nc.vector.memset(dump[:, 8:9], 0.0))

        @block.tensor
        def _(pe):
            pe.wait_ge(built, 2)
            pe.wait_ge(ident_r_in, 1)
            pe.wait_ge(dve_consts_in, 1)
            pe.wait_ge(weights_in, WEIGHTS)

            def mm(out, lhsT, rhs, start, stop):
                return nc.tensor.matmul(out, lhsT, rhs, start=start, stop=stop)

            def free_bank(b, name, m):
                k = JOB[name, m]
                if k < RING:
                    for e in "AD":
                        pe.wait_ge(freed[e], PER_B[e] * b + CREDIT)
                else:
                    wait_freed(pe, b, *JOBS[k - RING][0:2])
                return bank(name, m)

            def over_e(out, lhs, rhs):
                for e in range(EB):
                    last = mm(out, lhs(e), rhs(e), e == 0, e == EB - 1)
                return last

            def over_c(out, w, m, src):
                for e in range(CBN):
                    last = mm(out, w[0:CB[e], e, m * P:m * P + CB[m]], src[0:CB[e], e, :], e == 0, e == CBN - 1)
                return last

            def head_scores(b, l, n, pair, par, half):
                g = HEADS * b + n
                if half == 0:
                    pe.wait_ge(slots_in[l][par], SLOT_LOADS * (PAIRS * b + pair + 2))
                if l == 0:
                    pe.wait_ge(max_half[0], 2 * (g + 2) + half + CREDIT)
                else:
                    pe.wait_ge(p_chunk, SC * (g + 2) + 2 * half + CREDIT)
                for i in range(2):
                    c = 2 * half + i
                    last = mm(ps_s[:, i, :], q_slot[par][0:SCORE_ROWS, P * c:P * c + P], k_slot[l][par][0:SCORE_ROWS, :], True, True)
                last.then_inc(s_half[l], 1)

            def head_maxT(b, l, n, par):
                pe.wait_ge(max_half[l], 2 * (HEADS * b + n + 2) + CREDIT)
                for c in range(SC):
                    last = mm(ps_m[0:SHIFT_ROWS, P * c:P * c + P], row_max[l][1 - par][:, c, :], ident_r[:, :], True, True)
                last.then_inc(maxT_done[l], 1)

            def head_scoresT(b, l, n, par, half):
                g = HEADS * b + n
                if half == 0:
                    pe.wait_ge(shift_in[l], g + 2)
                pe.wait_ge(pt_half[l], 2 * (g + 1) + half + CREDIT)
                for i in range(2):
                    t = 2 * half + i
                    last = mm(ps_t[:, i, :], k_slot[l][1 - par][:, P * t:P * t + P], q_slot[1 - par][:, :], True, True)
                last.then_inc(st_half[l], 1)

            def step0(b, n, par, use, transposed, scores, pair):
                g = HEADS * b + n

                def out0(c):
                    for t in range(TB):
                        last = mm(ps_w[par][:, V0W * c:V0W * c + V0W], probsT[par][:, t, P * c:P * c + P], v0_sb[:, t, n, :],
                                  t == 0, t == TB - 1)
                    return last

                if transposed:
                    head_maxT(b, 0, n, par)
                if use:
                    pe.wait_ge(pt_half[0], 2 * (g + 1) + CREDIT)
                    pe.wait_ge(o_moved, g - 1 + CREDIT)
                    out0(0)
                    out0(1)
                if transposed:
                    head_scoresT(b, 0, n, par, 0)
                if use:
                    out0(2)
                if transposed:
                    head_scoresT(b, 0, n, par, 1)
                if scores:
                    head_scores(b, 0, n, pair, par, 0)
                if use:
                    out0(3).then_inc(o_done, 1)
                if scores:
                    head_scores(b, 0, n, pair, par, 1)

            def step1(b, n, par, use, transposed, scores, pair):
                g = HEADS * b + n

                def gram_product(c):
                    pe.wait_ge(z_done, SC * g + c - 1 + CREDIT)
                    out = ps_w[c % 2]
                    for t in range(TB):
                        rows = P if t < TB - 1 else P - IPN
                        lo = P * max(t, 1) - P
                        last = mm(out[:, lo:GW], probsT[par][0:rows, t, P * c:P * c + P], gram[par][0:rows, t, lo:GW],
                                  t == 0, t == TB - 1)
                    last.then_inc(w_done, 1)

                if transposed:
                    head_maxT(b, 1, n, par)
                if use:
                    pe.wait_ge(pt_half[1], 2 * (g + 1) + CREDIT)
                    pe.wait_ge(zb_done, g + CREDIT)
                    for c in range(SC):
                        last = mm(ps_b[:, P * c:P * c + P], probsT[par][:, 0, P * c:P * c + P], gram00[:, :], True, True)
                    last.then_inc(b_done, 1)
                    pe.wait_ge(v_in, g + 1)
                    gram_product(0)
                if transposed:
                    head_scoresT(b, 1, n, par, 0)
                if use:
                    gram_product(1)
                if transposed:
                    head_scoresT(b, 1, n, par, 1)
                if scores:
                    head_scores(b, 1, n, pair, par, 0)
                if use:
                    gram_product(2)
                if scores:
                    head_scores(b, 1, n, pair, par, 1)
                if use:
                    gram_product(3)

            def run_pe_heads(step, b):
                step(b, -2, 0, False, False, True, -1)
                step(b, -1, 1, False, True, True, -1)
                with pe.Fori(0, PAIRS - 1) as pair:
                    step(b, 2 * pair, 0, True, True, True, pair)
                    step(b, 2 * pair + 1, 1, True, True, True, pair)
                step(b, HEADS - 2, 0, True, True, False, PAIRS - 1)
                step(b, HEADS - 1, 1, True, False, False, PAIRS - 1)

            with pe.Fori(0, BATCH) as b:
                pe.wait_ge(ctx_in, 16 * b + 16)
                pe.wait_ge(x_in, 32 * b + 32)
                for m in range(CBN):
                    out, cols = free_bank(b, "k0", m), slice(m * P, m * P + CB[m])
                    over_e(out[0:CB[m], 0:TEXT0], lambda e: w_big["k0"][:, e, cols], lambda e: ctx_sb[:, e, 0:TEXT0])
                    over_e(out[0:CB[m], TEXT0:T], lambda e: w_big["ki0"][:, e, cols], lambda e: ctx_sb[:, e, TEXT0:T])\
                        .then_inc(job_done, 1)
                for m in range(CBN):
                    over_c(free_bank(b, "q0", m)[0:CB[m], :], w_small["q0"], m, x_sb).then_inc(job_done, 1)
                for m in range(CBN):
                    out, cols = free_bank(b, "k1", m), slice(m * P, m * P + CB[m])
                    over_e(out[0:CB[m], 0:TEXT1], lambda e: w_big["k1"][:, e, cols], lambda e: ctx_sb[:, e, 0:TEXT1])
                    over_e(out[0:CB[m], TEXT1:T], lambda e: w_big["ki1"][:, e, cols], lambda e: ctx_sb[:, e, TEXT1:T])\
                        .then_inc(job_done, 1)
                out = free_bank(b, "v0t", 0)
                over_e(out[0:TEXT0, 0:C], lambda e: ctx_sb[:, e, 0:TEXT0], lambda e: w_big["v0"][:, e, :]).then_inc(job_done, 1)
                for t in range(TB):
                    out = free_bank(b, "v0i", t)
                    over_e(out[:, 0:C], lambda e: ctx_sb[:, e, P * t:P * t + P], lambda e: w_big["vi0"][:, e, :])\
                        .then_inc(job_done, 1)
                for i in range(TB):
                    out = free_bank(b, "g", i)
                    over_e(out[:, 0:T - P * i], lambda e: ctx_sb[:, e, P * i:P * i + P], lambda e: ctx_sb[:, e, P * i:T])\
                        .then_inc(job_done, 1)
                for t in range(TB):
                    out = free_bank(b, "v1", t)
                    over_e(out[:, 0:C], lambda e: ctx_sb[:, e, P * t:P * t + P], lambda e: w_big["v1"][:, e, :])\
                        .then_inc(job_done, 1)
                pe.wait_ge(ip_sq_in, b + 1)
                over_e(free_bank(b, "ipn", 0)[:, 0:IPN], lambda e: ones[:, :], lambda e: ip_sq[:, e, :]).then_inc(job_done, 1)
                over_e(free_bank(b, "vip", 0)[0:IPN, 0:C], lambda e: ctx_sb[:, e, TEXT1:T], lambda e: w_big["vi1"][:, e, :])\
                    .then_inc(job_done, 1)
                wait_freed(pe, b, "vip", 0)
                for i in range(IPN):
                    mm(free_bank(b, "vrep", i)[:, 0:C], pick[:, i, :], vip[:, :], True, True).then_inc(job_done, 1)
                wait_freed(pe, b, "vrep", IPN - 1)
                run_pe_heads(step0, b)

                def transposed_heads(name, l):
                    pe.wait_ge(heads_ready, 2 * b + l + 1)
                    for m in range(CBN):
                        out = free_bank(b, name, m)
                        pe.sem_inc(passed, 1)
                        for c in range(SC):
                            last = nc.tensor.transpose(out[0:CB[m], P * c:P * c + P], heads_out[:, c, P * m:P * m + CB[m]],
                                                       ident[:, :])
                        last.then_inc(job_done, 1)

                transposed_heads("tr0", 0)
                wait_freed(pe, b, "tr0", CBN - 1)
                for m in range(CBN):
                    over_c(free_bank(b, "x1", m)[0:CB[m], :], w_small["o0"], m, heads_outT).then_inc(job_done, 1)
                wait_freed(pe, b, "x1", CBN - 1)
                for m in range(CBN):
                    over_c(free_bank(b, "q1", m)[0:CB[m], :], w_small["q1"], m, x1_sb).then_inc(job_done, 1)
                wait_freed(pe, b, "q1", CBN - 1)
                pe.wait_ge(gram_copied, b + 1)
                run_pe_heads(step1, b)
                transposed_heads("tr1", 1)
                wait_freed(pe, b, "tr1", CBN - 1)
                for m in range(CBN):
                    over_c(free_bank(b, "y", m)[0:CB[m], :], w_small["o1"], m, heads_outT).then_inc(job_done, 1)


def kernel(x, ctx_2048, fside_S_0, L0_xattn_Wq, L0_xattn_Wk, L0_xattn_Wv, L0_xattn_Wk_ip, L0_xattn_Wv_ip, L0_xattn_Wo,
           L0_xattn_bo, L1_xattn_W_q, L1_xattn_W_k, L1_xattn_W_v, L1_xattn_W_k_ip, L1_xattn_W_v_ip, L1_xattn_W_out,
           L1_xattn_b_out):
    import numpy as np
    import concourse.bacc as bacc
    from concourse.bass_utils import run_bass_kernel_spmd

    given = {
        "xT": np.asarray(x).transpose(0, 2, 1),
        "ctxT": np.asarray(ctx_2048).transpose(0, 2, 1),
        "mask": np.asarray(fside_S_0).reshape(SC, P).T,
        "wq0": np.asarray(L0_xattn_Wq).T,
        "wk0": np.asarray(L0_xattn_Wk).T,
        "wv0": np.asarray(L0_xattn_Wv).T,
        "wki0": np.asarray(L0_xattn_Wk_ip).T,
        "wvi0": np.asarray(L0_xattn_Wv_ip).T,
        "wo0": np.asarray(L0_xattn_Wo).T,
        "bo0": np.asarray(L0_xattn_bo).reshape(C, 1),
        "wq1": np.asarray(L1_xattn_W_q),
        "wk1": np.asarray(L1_xattn_W_k),
        "wv1": np.asarray(L1_xattn_W_v),
        "wki1": np.asarray(L1_xattn_W_k_ip),
        "wvi1": np.asarray(L1_xattn_W_v_ip),
        "wo1": np.asarray(L1_xattn_W_out),
        "bo1": np.asarray(L1_xattn_b_out).reshape(C, 1),
    }
    nc = bacc.Bacc("TRN2", target_bir_lowering=False, num_devices=1)
    arrays, args = {}, []
    for name, a in given.items():
        a = np.ascontiguousarray(a)
        arrays[f"in_{name}"] = a
        args.append(nc.dram_tensor(f"in_{name}", a.shape, mybir.dt.from_np(a.dtype), kind="ExternalInput").ap())
    out = nc.dram_tensor("outT", [BATCH, C, S], F32, kind="ExternalOutput").ap()
    build(nc, *args, out)
    r = run_bass_kernel_spmd(nc, [arrays], core_ids=[0])
    return np.ascontiguousarray(r.results[0]["outT"].transpose(0, 2, 1))
```

```python
from contextlib import ExitStack

import concourse.bass as bass
from concourse import mybir

ACT = mybir.ActivationFunctionType
ALU = mybir.AluOpType
AX = mybir.AxisListType
F32 = mybir.dt.float32
F32R = mybir.dt.float32r

P = 128
BATCH, S, C, E, T = 4, 512, 320, 512, 512
HEADS, D = 20, 16

TEXT0 = 77
IPN = 4
TEXT1 = T - IPN
SCALE = float(D) ** -0.5
SEM_SCALE = 0.5
EPS = 1e-12
SC = S // P
TB = T // P
EB = E // P
CB = [P, P, C - 2 * P]
CBN = len(CB)

PART = D
SCORE_ROWS = 3 * PART
SHIFT_ROW = 64
SHIFT_ROWS = 33
ALL_ROWS = SHIFT_ROW + SHIFT_ROWS
SLOTS = 4
TURNS = HEADS // SLOTS
SLOT_LOADS = 6 * 16

V0W = 2 * (D + 1)
GA = T - P
GW = GA + D
GN = TEXT1 - P
OUT1 = 24
A1, V1, NA, NB = 0, IPN, IPN + D, IPN + D + 1
SZW = 8

NEXT = (
    [("v0t", 0, "A")]
    + [("v0i", t, "A") for t in range(TB)]
    + [("k0", m, "D") for m in range(CBN)]
    + [("q0", m, "D") for m in range(CBN)]
)
JOBS = (
    [("k1", m, "D") for m in range(CBN)]
    + [("g", i, "A") for i in range(TB)]
    + [("tr0", m, "A") for m in range(CBN)]
    + [("x1", m, "D") for m in range(CBN)]
    + [("q1", m, "D") for m in range(CBN)]
    + [("v1", t, "A") for t in range(TB)]
    + [("ipn", 0, "D"), ("vip", 0, "D")]
    + [("vrep", n, "D") for n in range(IPN)]
    + NEXT
    + [("tr1", m, "A") for m in range(CBN)]
    + [("y", m, "D") for m in range(CBN)]
)
JOB = {(name, m): k for k, (name, m, _) in enumerate(JOBS)}
FIRST_NEXT = JOB["v0t", 0]
FREED_BY = [e for _, _, e in JOBS]
BEFORE = {e: [x for _, _, x in NEXT].count(e) for e in "AD"}
PER_B = {e: FREED_BY.count(e) for e in "AD"}
HIGHS = ("k1", "q1", "k0", "q0")
FIRST = "first"
RING = 4
WEIGHTS = 16 * (8 + 8 + 2 * CBN + 1)
CREDIT = 8


def build(nc, xT, ctxT, mask, wq0, wk0, wv0, wki0, wvi0, wo0, bo0, wq1, wk1, wv1, wki1, wvi1, wo1, bo1, outT):
    with ExitStack() as ctx:
        def sb(name, shape, dt=F32):
            return ctx.enter_context(nc.sbuf_tensor(name, shape, dt))

        def sem(name):
            return ctx.enter_context(nc.semaphore(name))

        scratch = {n: nc.dram_tensor(f"parts_{n}", [2, HEADS, D, S], F32, kind="Internal").ap()
                   for n in ("k0", "q0", "k1", "q1")}

        w_small = {n: sb(f"w_{n}", [P, CBN, C]) for n in ("q0", "o0", "q1", "o1")}
        w_big = {n: sb(f"w_{n}", [P, EB, C]) for n in ("k0", "v0", "ki0", "vi0", "k1", "v1", "ki1", "vi1")}
        bias_o = [sb(f"bias_o{l}", [P, CBN]) for l in range(2)]
        mask_sb = sb("mask_sb", [P, SC])
        ctx_sb = sb("ctx_sb", [P, EB, T])
        x_sb = sb("x_sb", [P, CBN, S])
        x1_sb = sb("x1_sb", [P, CBN, S])
        ident = sb("ident", [P, P])
        ident_r = sb("ident_r", [P, P], F32R)
        ones = sb("ones", [P, P])
        pick = sb("pick", [IPN, IPN, P])
        ip_rows = sb("ip_rows", [P, 1])
        v0_sb = sb("v0_sb", [P, TB, HEADS, V0W])
        v1_sb = sb("v1_sb", [P, TB, C])
        gram00 = sb("gram00", [P, P])
        gram = [sb(f"gram{p}", [P, TB, GW]) for p in range(2)]
        ip_sq = sb("ip_sq", [P, EB, IPN])
        v0_slot = [sb(f"v0_slot{p}", [P, TB, V0W]) for p in range(2)]
        vip = sb("vip", [IPN, C])
        vip_rep = sb("vip_rep", [P, IPN, C])
        q_slot = [sb(f"q_slot{i}", [ALL_ROWS, S], F32R) for i in range(SLOTS)]
        k_slot = [sb(f"k_slot{i}", [ALL_ROWS, T], F32R) for i in range(SLOTS)]
        row_max = [[sb(f"row_max{l}{p}", [P, SC, SHIFT_ROWS if l == 0 else 1], F32R) for p in range(2)] for l in range(2)]
        probsT = [sb(f"probsT{p}", [P, TB, S]) for p in range(2)]
        probs = [sb(f"probs{p}", [P, SC, S]) for p in range(2)]
        parts_q = sb("parts_q", [P, 2, CBN, S])
        exp_bias = [sb(f"exp_bias{p}", [P, SC]) for p in range(2)]
        sz = [sb(f"sz{p}", [P, SC, SZW]) for p in range(2)]
        head_out = [sb(f"head_out{p}", [P, SC, OUT1]) for p in range(2)]
        out_all = sb("out_all", [P, HEADS * SC * V0W])
        o0_all = out_all[:, :].rearrange("p (h c w) -> p h c w", h=HEADS, c=SC)
        o1_all = out_all[:, 0:HEADS * SC * OUT1].rearrange("p (h c w) -> p h c w", h=HEADS, c=SC)
        sz_all = sb("sz_all", [P, HEADS, SC, SZW])
        dump = sb("dump", [P, 64])
        heads_out = sb("heads_out", [P, SC, C])
        heads_outT = sb("heads_outT", [P, CBN, S])
        outT0 = [heads_outT[0:V0W, p, :] for p in range(2)]
        nd = HEADS * SC
        stat = sb("stat", [P, nd, 8])
        root = sb("root", [P, nd + IPN])
        ip_norm2 = sb("ip_norm2", [P, IPN])
        rip = sb("rip", [P, IPN])
        fused = sb("fused", [P, nd, IPN])
        wide = [probs[i][:, :, :].rearrange("p c s -> p (c s)")[:, 0:nd * D].rearrange("p (n d) -> p n d", d=D)
                for i in range(2)]
        parts = {"k0": [probsT[0][:, 0:CBN, :], probsT[1][:, 0:CBN, :]],
                 "k1": [probsT[0][:, 0:CBN, :], probsT[1][:, 0:CBN, :]],
                 "q0": [parts_q[:, 0, :, :], parts_q[:, 1, :, :]],
                 "q1": [parts_q[:, 0, :, :], parts_q[:, 1, :, :]]}


        ps_s = ctx.enter_context(nc.psum_tensor("ps_s", [P, 2, 512], F32))
        ps_t = ctx.enter_context(nc.psum_tensor("ps_t", [P, 2, 512], F32))
        ps_w = [ctx.enter_context(nc.psum_tensor(f"ps_w{i}", [P, 512], F32)) for i in range(2)]
        ps_b = ctx.enter_context(nc.psum_tensor("ps_b", [P, 512], F32))
        ps_m = ctx.enter_context(nc.psum_tensor("ps_m", [P, 512], F32))
        ring = [ps_s[:, 0, :], ps_s[:, 1, :], ps_t[:, 0, :], ps_t[:, 1, :]]

        weights_in = sem("weights_in")
        filled, built = sem("filled"), sem("built")
        ident_r_in = sem("ident_r_in")
        dve_consts_in = sem("dve_consts_in")
        ctx_in, x_in = sem("ctx_in"), sem("x_in")
        job_done = sem("job_done")
        freed = {"A": sem("freed_by_act"), "D": sem("freed_by_dve")}
        high_in = sem("high_in")
        ip_sq_in = sem("ip_sq_in")
        gram_copied = sem("gram_copied")
        stored = {n: sem(f"stored_{n}") for n in scratch}
        y_out = sem("y_out")
        passed = sem("passed")
        heads_ready = sem("heads_ready")
        chain = sem("chain")
        ask_root, root_in = sem("ask_root"), sem("root_in")
        ask_exp, exp_in = sem("ask_exp"), sem("exp_in")
        slots_in = [[sem(f"slots_in{l}{i}") for i in range(SLOTS)] for l in range(2)]
        s_half = [sem(f"s_half{l}") for l in range(2)]
        max_half = [sem(f"max_half{l}") for l in range(2)]
        maxT_done = [sem(f"maxT_done{l}") for l in range(2)]
        shift_in = [sem(f"shift_in{l}") for l in range(2)]
        st_half = [sem(f"st_half{l}") for l in range(2)]
        pt_half = [sem(f"pt_half{l}") for l in range(2)]
        v0_in = sem("v0_in")
        oT_done = sem("oT_done")
        oT_moved = sem("oT_moved")
        o_done = sem("o_done")
        o_moved = sem("o_moved")
        bias_in = sem("bias_in")
        p_chunk = sem("p_chunk")
        v_in = sem("v_in")
        b_done, w_done = sem("b_done"), sem("w_done")
        zb_done, z_done = sem("zb_done"), sem("z_done")
        sz_moved, out_moved = sem("sz_moved"), sem("out_moved")

        def left_out(b, k):
            return b == BATCH - 1 if isinstance(b, int) and k > FIRST_NEXT else False

        def jobs_done(b, k):
            if b is FIRST:
                return k - FIRST_NEXT
            return len(JOBS) * b + k + (0 if left_out(b, k) else len(NEXT))

        def freed_value(b, e, k):
            if b is FIRST:
                return CREDIT + FREED_BY[FIRST_NEXT:k].count(e)
            return PER_B[e] * b + CREDIT + FREED_BY[:k].count(e) + (0 if left_out(b, k) else BEFORE[e])

        def wait_freed(eng, b, name, m):
            k = JOB[name, m]
            e = FREED_BY[k]
            eng.wait_ge(freed[e], freed_value(b, e, k + 1))

        def wait_job(eng, b, name, m):
            eng.wait_ge(job_done, jobs_done(b, JOB[name, m] + 1))

        def bank(name, m):
            return ring[JOB[name, m] % RING]

        def run_batches(eng, batch):
            with eng.Fori(0, BATCH - 1) as b:
                batch(b, True)
            batch(BATCH - 1, False)

        def run_heads(step, eng, b):
            step(b, -2, SLOTS - 2, -1, False, False, True)
            step(b, -1, SLOTS - 1, -1, False, True, True)
            with eng.Fori(0, TURNS - 1) as turn:
                for k in range(SLOTS):
                    step(b, SLOTS * turn + k, k, turn, True, True, True)
            for k in range(SLOTS):
                step(b, HEADS - SLOTS + k, k, TURNS - 1, True, k < SLOTS - 1, k < SLOTS - 2)

        def load_inputs(eng, batch):
            eng.dma_start(ctx_sb[:, :, :], ctxT[batch, :, :].rearrange("(k p) t -> p k t", p=P)).then_inc(ctx_in, 16)
            eng.dma_start(x_sb[:, 0:2, :], xT[batch, 0:2 * P, :].rearrange("(k p) s -> p k s", p=P)).then_inc(x_in, 16)
            eng.dma_start(x_sb[0:CB[2], 2, :], xT[batch, 2 * P:C, :]).then_inc(x_in, 16)

        block = ctx.enter_context(nc.Block())

        @block.sync
        def _(sp):
            load_inputs(sp, 0)
            for n, src in (("k0", wk0), ("ki0", wki0), ("v0", wv0), ("vi0", wvi0),
                           ("k1", wk1), ("ki1", wki1), ("v1", wv1), ("vi1", wvi1)):
                sp.dma_start(w_big[n][:, :, :], src.rearrange("(k p) n -> p k n", p=P)).then_inc(weights_in, 16)
            for n, src in (("q0", wq0), ("o0", wo0), ("q1", wq1), ("o1", wo1)):
                sp.dma_start(w_small[n][:, 0:2, :], src[0:2 * P, :].rearrange("(k p) n -> p k n", p=P)).then_inc(weights_in, 16)
                sp.dma_start(w_small[n][0:CB[2], 2, :], src[2 * P:C, :]).then_inc(weights_in, 16)
            for l, src in ((0, bo0), (1, bo1)):
                for m in range(CBN):
                    sp.dma_start(bias_o[l][0:CB[m], m:m + 1], src[m * P:m * P + CB[m], :]).then_inc(weights_in, 16)
            sp.dma_start(mask_sb[:, :], mask).then_inc(weights_in, 16)

            def store(b, name):
                for part in range(2):
                    dst = scratch[name][part, :, :, :].rearrange("h d s -> (h d) s")
                    sp.dma_start(dst[0:2 * P, :].rearrange("(k p) s -> p k s", p=P),
                                 parts[name][part][:, 0:2, :]).then_inc(stored[name], 16)
                    sp.dma_start(dst[2 * P:C, :], parts[name][part][0:CB[2], 2, :]).then_inc(stored[name], 16)

            def load_slots(b, l, n, k):
                qs, ks = scratch[f"q{l}"], scratch[f"k{l}"]
                sp.wait_ge(pt_half[l], 2 * (HEADS * b + n - SLOTS + 1) + CREDIT)
                for i, (qp, kp) in enumerate(((0, 0), (0, 1), (1, 0))):
                    rows = slice(PART * i, PART * i + PART)
                    sp.dma_start(q_slot[k][rows, :].bitcast(F32), qs[qp, n, :, :]).then_inc(slots_in[l][k], 16)
                    sp.dma_start(k_slot[k][rows, :].bitcast(F32), ks[kp, n, :, :]).then_inc(slots_in[l][k], 16)

            def load_all(b, l):
                with sp.Fori(0, TURNS) as turn:
                    for k in range(SLOTS):
                        load_slots(b, l, SLOTS * turn + k, k)

            def split_and_loaded(b, batch, l, names):
                for name in names:
                    wait_freed(sp, b, name, CBN - 1)
                    store(b, name)
                for name in names:
                    sp.wait_ge(stored[name], 64 * (batch + 1))
                sp.sem_inc(passed, 1)
                load_all(batch, l)

            split_and_loaded(FIRST, 0, 0, ("k0", "q0"))
            with sp.Fori(0, BATCH - 1) as b:
                split_and_loaded(b, b, 1, ("k1", "q1"))
                split_and_loaded(b, b + 1, 0, ("k0", "q0"))
            split_and_loaded(BATCH - 1, BATCH - 1, 1, ("k1", "q1"))

        @block.gpsimd
        def _(pool):
            nc.gpsimd.memset(ident[:, :], 0.0).then_inc(filled, 1)
            nc.gpsimd.memset(pick[:, :, :], 0.0).then_inc(filled, 1)
            nc.gpsimd.memset(ones[:, :], 1.0).then_inc(filled, 1)
            nc.gpsimd.memset(out_all[:, 0:1], 0.0).then_inc(out_moved, CREDIT)
            pool.wait_ge(filled, 3)
            nc.gpsimd.affine_select(out=ident[:, :], in_=ident[:, :], compare_op=ALU.not_equal, fill=1.0, base=0,
                                    pattern=[[-1, P]], channel_multiplier=1).then_inc(built, 1)
            nc.gpsimd.affine_select(out=pick[:, :, :], in_=pick[:, :, :], compare_op=ALU.not_equal, fill=1.0, base=0,
                                    pattern=[[-1, IPN], [0, P]], channel_multiplier=1).then_inc(built, 1)

            def step0(b, n, k, turn, use, transposed, scores):
                par = k % 2
                if scores:
                    pool.wait_ge(oT_moved, HEADS * b + n + 1 + CREDIT) if use else None
                    pool.sem_inc(passed, 1)
                    nc.gpsimd.tensor_copy(v0_slot[par][:, :, :], v0_sb[:, :, n + 2, :]).then_inc(v0_in, 1)

            def step1(b, n, k, turn, use, transposed, scores):
                par = k % 2
                g = HEADS * b + n
                if scores:
                    for half in range(2):
                        pool.wait_ge(max_half[1], 2 * (g + 2) + half + 1 + CREDIT)
                        pool.sem_inc(passed, 1)
                        nc.gpsimd.tensor_scalar_mul(exp_bias[par][:, 2 * half:2 * half + 2],
                                                    row_max[1][par][:, 2 * half:2 * half + 2, 0].bitcast(F32), -SCALE)\
                            .then_inc(bias_in, 1)
                if use:
                    pool.wait_ge(z_done, SC * (g + 1) + CREDIT)
                    pool.sem_inc(passed, 1)
                    nc.gpsimd.tensor_copy(o1_all[:, n, :, 0:OUT1 - 2], head_out[par][:, :, 0:OUT1 - 2]).then_inc(out_moved, 1)
                if scores:
                    nc.gpsimd.tensor_copy(gram[par][:, :, GA:GW], v1_sb[:, :, :].rearrange("p t (h d) -> p t h d", d=D)[:, :, n + 2, :])\
                        .then_inc(v_in, 1)
                    pool.wait_ge(p_chunk, SC * (g + 3) + CREDIT)
                    pool.sem_inc(passed, 1)
                    nc.gpsimd.tensor_copy(sz_all[:, n + 2, :, 0:IPN + 1], sz[par][:, :, 0:IPN + 1]).then_inc(sz_moved, 1)

            wait_freed(pool, FIRST, "v0i", TB - 1)
            pool.sem_inc(passed, 1)

            def batch(b, ahead):
                run_heads(step0, pool, b)
                wait_freed(pool, b, "g", TB - 1)
                pool.sem_inc(passed, 1)
                for i in range(TB):
                    lo = P * max(i, 1) - P
                    last = nc.gpsimd.tensor_copy(gram[1][:, i, lo:GA], gram[0][:, i, lo:GA])
                last.then_inc(gram_copied, 1)
                wait_freed(pool, b, "v1", TB - 1)
                pool.sem_inc(passed, 1)
                run_heads(step1, pool, b)
                if ahead:
                    wait_freed(pool, b, "v0i", TB - 1)
                    pool.sem_inc(passed, 1)

            run_batches(pool, batch)

        @block.scalar
        def _(act):
            act.wait_ge(built, 2)
            nc.scalar.activation(ident_r[:, :], ident[:, :], ACT.Copy).then_inc(ident_r_in, 1)
            for i, s in enumerate((freed["A"], pt_half[0], pt_half[1], oT_moved, p_chunk)):
                nc.scalar.activation(dump[:, i:i + 1], ident[:, 0:1], ACT.Copy).then_inc(s, CREDIT)
            act.wait_ge(dve_consts_in, 1)

            def high(b, name, m):
                wait_job(act, b, name, m)
                nc.scalar.activation(parts[name][0][0:CB[m], m, :].bitcast(F32R), bank(name, m)[0:CB[m], :],
                                     ACT.Copy).then_inc(high_in, 1)

            def shift(b, l, n, k):
                act.wait_ge(maxT_done[l], HEADS * b + n + 2)
                nc.scalar.activation(q_slot[(k + 1) % SLOTS][SHIFT_ROW:ALL_ROWS, :], ps_m[0:SHIFT_ROWS, :], ACT.Copy)\
                    .then_inc(shift_in[l], 1)

            def expT(b, l, n, par, half):
                act.wait_ge(st_half[l], 2 * (HEADS * b + n + 1) + half + 1)
                nc.scalar.activation(probsT[1 - par][:, 2 * half:2 * half + 2, :], ps_t[:, :, :], ACT.Exp,
                                     scale=SCALE).then_inc(pt_half[l], 1)

            def step0(b, n, k, turn, use, transposed, scores):
                par = k % 2
                if transposed:
                    shift(b, 0, n, k)
                    expT(b, 0, n, par, 0)
                if use:
                    act.wait_ge(oT_done, HEADS * b + n + 1)
                    nc.scalar.activation(outT0[par], ps_w[par][0:V0W, :], ACT.Copy).then_inc(oT_moved, 1)
                if transposed:
                    expT(b, 0, n, par, 1)

            def step1(b, n, k, turn, use, transposed, scores):
                par = k % 2
                g = HEADS * b + n
                if transposed:
                    shift(b, 1, n, k)
                    expT(b, 1, n, par, 0)
                    expT(b, 1, n, par, 1)
                if scores:
                    for c in range(SC):
                        if c % 2 == 0:
                            act.wait_ge(bias_in, 2 * (g + 2) + c // 2 + 1)
                        act.wait_ge(z_done, SC * g + c + 1 + CREDIT) if use else None
                        nc.scalar.activation(probs[par][:, c, 0:TEXT1], ps_s[:, c % 2, 0:TEXT1], ACT.Exp,
                                             bias=exp_bias[par][:, c:c + 1], scale=SCALE,
                                             accum_out=sz[par][:, c, IPN:IPN + 1]).then_inc(p_chunk, 1)

            def v0_text(b):
                wait_job(act, b, "v0t", 0)
                nc.scalar.activation(v0_sb[0:TEXT0, 0, :, 0:D],
                                     bank("v0t", 0)[0:TEXT0, 0:C].rearrange("p (h d) -> p h d", d=D),
                                     ACT.Copy).then_inc(freed["A"], 1)

            def v0_ip(b, t):
                wait_job(act, b, "v0i", t)
                nc.scalar.activation(v0_sb[:, t, :, D + 1:2 * D + 1],
                                     bank("v0i", t)[:, 0:C].rearrange("p (h d) -> p h d", d=D),
                                     ACT.Copy, scale=ip_rows[:, :] if t == 0 else 1.0).then_inc(freed["A"], 1)

            def gram_rows(b, i):
                wait_job(act, b, "g", i)
                src = bank("g", i)
                diag = P if i < TB - 1 else P - IPN
                dst = gram00[:, :] if i == 0 else gram[0][:, i, P * (i - 1):P * (i - 1) + diag]
                nc.scalar.activation(dst, src[:, 0:diag], ACT.Copy)
                nc.scalar.activation(gram[0][:, i, P * i - P + diag:GA], src[:, diag:T - P * i], ACT.Copy, scale=2.0)\
                    .then_inc(freed["A"], 1)

            def move_transposed(b, name):
                for m in range(CBN):
                    wait_job(act, b, name, m)
                    nc.scalar.activation(heads_outT[0:CB[m], m, :], bank(name, m)[0:CB[m], :], ACT.Copy).then_inc(freed["A"], 1)

            def highs(b, name):
                for m in range(CBN):
                    high(b, name, m)

            def batch(b, ahead):
                run_heads(step0, act, b)
                highs(b, "k1")
                for i in range(TB):
                    gram_rows(b, i)
                move_transposed(b, "tr0")
                highs(b, "q1")
                for t in range(TB):
                    wait_job(act, b, "v1", t)
                    nc.scalar.activation(v1_sb[:, t, :], bank("v1", t)[:, 0:C], ACT.Copy).then_inc(freed["A"], 1)
                if ahead:
                    wait_freed(act, b, "vip", 0)
                    load_inputs(act, b + 1)
                run_heads(step1, act, b)
                if ahead:
                    v0_text(b)
                act.wait_ge(ask_root, b + 1)
                nc.scalar.activation(root[:, :], root[:, :], ACT.Sqrt).then_inc(root_in, 1)
                if ahead:
                    v0_ip(b, 0)
                    v0_ip(b, 1)
                act.wait_ge(ask_exp, b + 1)
                nc.scalar.activation(fused[:, :, :], fused[:, :, :], ACT.Exp).then_inc(exp_in, 1)
                if ahead:
                    v0_ip(b, 2)
                    v0_ip(b, 3)
                    highs(b, "k0")
                    highs(b, "q0")
                move_transposed(b, "tr1")
                for m in range(CBN):
                    wait_freed(act, b, "y", m)
                    act.dma_start(outT[b, m * P:m * P + CB[m], :], x1_sb[0:CB[m], m, :]).then_inc(y_out, 16)

            v0_text(FIRST)
            for t in range(TB):
                v0_ip(FIRST, t)
            highs(FIRST, "k0")
            highs(FIRST, "q0")
            run_batches(act, batch)
            act.wait_ge(y_out, 16 * CBN * BATCH + 16)

        @block.vector
        def _(dve):
            for i, s in enumerate((freed["D"], max_half[0], max_half[1], z_done, zb_done, o_moved)):
                nc.vector.memset(stat[:, i, 0:1], 0.0).then_inc(s, CREDIT)
            nc.vector.memset(stat[:, 6, 0:1], 0.0).then_inc(y_out, 16)
            zero = [t[:, :] for t in q_slot + k_slot] + [t[:, :, :] for t in row_max[0] + row_max[1]]
            for t in zero:
                nc.vector.memset(t.bitcast(F32), 0.0)
            nc.vector.memset(v0_sb[:, :, :, :], 0.0)
            nc.vector.memset(ip_rows[:, :], 1.0)
            nc.vector.memset(dump[:, 8:9], 0.0).then_inc(chain, 1)
            dve.wait_ge(chain, 1)
            for slot in k_slot:
                nc.vector.memset(slot[SHIFT_ROW:SHIFT_ROW + 1, 0:TEXT0].bitcast(F32), -1.0)
                nc.vector.memset(slot[ALL_ROWS - 1:ALL_ROWS, TEXT0:T].bitcast(F32), -1.0)
            nc.vector.memset(ip_rows[0:TEXT0, :], 0.0)
            nc.vector.memset(v0_sb[:, :, :, 2 * D + 1:V0W], 1.0)
            nc.vector.memset(v0_sb[0:TEXT0, 0, :, D:D + 1], 1.0).then_inc(chain, 1)
            dve.wait_ge(chain, 2)
            nc.vector.memset(v0_sb[0:TEXT0, 0, :, 2 * D + 1:V0W], 0.0).then_inc(dve_consts_in, 1)
            CHAIN0 = 2
            links = [0]
            CHAIN_B = 26

            def link(b, ins):
                links[0] += 1
                ins.then_inc(chain, 1)
                dve.wait_ge(chain, CHAIN_B * b + links[0] + CHAIN0)

            def low(b, name, m):
                wait_job(dve, b, name, m)
                k = HIGHS.index(name) * CBN + m
                dve.wait_ge(high_in, k - 2 * CBN + 1 if b is FIRST else 4 * CBN * b + 2 * CBN + k + 1)
                nc.vector.tensor_tensor(parts[name][1][0:CB[m], m, :], bank(name, m)[0:CB[m], :],
                                        parts[name][0][0:CB[m], m, :], ALU.subtract).then_inc(freed["D"], 1)

            def step0(b, n, k, turn, use, transposed, scores):
                par = k % 2
                if scores:
                    for half in range(2):
                        cs = slice(2 * half, 2 * half + 2)
                        dve.wait_ge(s_half[0], 2 * (HEADS * b + n + 2) + half + 1)
                        nc.vector.tensor_reduce(out=row_max[0][par][:, cs, 0:1], in_=ps_s[:, :, 0:TEXT0], axis=AX.X, op=ALU.max)
                        nc.vector.tensor_reduce(out=row_max[0][par][:, cs, SHIFT_ROWS - 1:SHIFT_ROWS], in_=ps_s[:, :, TEXT0:T],
                                                axis=AX.X, op=ALU.max).then_inc(max_half[0], 1)
                if use:
                    dve.wait_ge(o_done, HEADS * b + n + 1)
                    nc.vector.tensor_copy(o0_all[:, n, :, :], ps_b[:, 0:SC * V0W].rearrange("p (c w) -> p c w", c=SC))\
                        .then_inc(o_moved, 1)

            def step1(b, n, k, turn, use, transposed, scores):
                par = k % 2
                g = HEADS * b + n

                def maxima(half):
                    cs = slice(2 * half, 2 * half + 2)
                    if half == 0:
                        dve.wait_ge(sz_moved, g + 1) if use else None
                    dve.wait_ge(s_half[1], 2 * (g + 2) + half + 1)
                    nc.vector.tensor_copy(sz[par][:, cs, 0:IPN], ps_s[:, :, TEXT1:T])
                    nc.vector.tensor_reduce(out=row_max[1][par][:, cs, 0:1], in_=ps_s[:, :, 0:TEXT1], axis=AX.X,
                                            op=ALU.max).then_inc(max_half[1], 1)

                if not use:
                    if scores:
                        maxima(0)
                        maxima(1)
                    return
                out = head_out[par]
                dve.wait_ge(b_done, g + 1)
                dve.wait_ge(p_chunk, SC * (g + 1) + CREDIT)
                dve.wait_ge(out_moved, g - 1 + CREDIT)
                for c in range(SC):
                    last = nc.vector.tensor_tensor_reduce(out=probs[par][:, c, 0:P], in0=ps_b[:, P * c:P * c + P], in1=probs[par][:, c, 0:P],
                                                          scale=1.0, scalar=0.0, op0=ALU.mult, op1=ALU.add,
                                                          accum_out=out[:, c, NB:NB + 1])
                last.then_inc(zb_done, 1)
                for c in range(SC):
                    if scores and c in (1, 3):
                        maxima(c // 2)
                    dve.wait_ge(w_done, SC * g + c + 1)
                    nc.vector.tensor_copy(out[:, c, 0:IPN + D], ps_w[c % 2][:, GN:GW])
                    nc.vector.tensor_tensor_reduce(out=probs[par][:, c, P:TEXT1], in0=ps_w[c % 2][:, 0:GN], in1=probs[par][:, c, P:TEXT1],
                                                   scale=1.0, scalar=0.0, op0=ALU.mult, op1=ALU.add,
                                                   accum_out=out[:, c, NA:NA + 1]).then_inc(z_done, 1)

            def lows(b, name):
                for m in range(CBN):
                    low(b, name, m)

            def batch(b, ahead):
                links[0] = 0
                run_heads(step0, dve, b)
                dve.wait_ge(o_moved, HEADS * (b + 1) + CREDIT)
                o0 = out_all[:, :].rearrange("p (n w) -> p n w", w=V0W)
                zr = stat[:, :, 0:2]
                link(b, nc.vector.reciprocal(zr, o0.rearrange("p n (a w) -> p n a w", a=2)[:, :, :, D]))
                nc.vector.tensor_tensor(wide[0], o0[:, :, 0:D], stat[:, :, 0:1].to_broadcast([P, nd, D]), ALU.mult)
                link(b, nc.vector.tensor_tensor(wide[1], o0[:, :, D + 1:2 * D + 1], stat[:, :, 1:2].to_broadcast([P, nd, D]), ALU.mult))
                by_head = heads_out[:, :, :].rearrange("p c (h d) -> p h c d", d=D)
                w4 = [w.rearrange("p (h c) d -> p h c d", c=SC) for w in wide]
                nc.vector.tensor_tensor(by_head, w4[0], w4[1], ALU.add).then_inc(heads_ready, 1)
                lows(b, "k1")
                dve.wait_ge(ctx_in, 16 * b + 16)
                nc.vector.tensor_tensor(ip_sq[:, :, :], ctx_sb[:, :, TEXT1:T], ctx_sb[:, :, TEXT1:T], ALU.mult)\
                    .then_inc(ip_sq_in, 1)
                dve.wait_ge(y_out, 16 * CBN * b + 16)
                for m in range(CBN):
                    wait_job(dve, b, "x1", m)
                    nc.vector.scalar_tensor_tensor(out=x1_sb[0:CB[m], m, :], in0=bank("x1", m)[0:CB[m], :],
                                                   scalar=bias_o[0][0:CB[m], m:m + 1], in1=x_sb[0:CB[m], m, :],
                                                   op0=ALU.add, op1=ALU.add).then_inc(freed["D"], 1)
                lows(b, "q1")
                wait_job(dve, b, "ipn", 0)
                nc.vector.tensor_copy(ip_norm2[:, :], bank("ipn", 0)[:, 0:IPN]).then_inc(freed["D"], 1)
                wait_job(dve, b, "vip", 0)
                nc.vector.tensor_copy(vip[:, :], bank("vip", 0)[0:IPN, 0:C]).then_inc(freed["D"], 1)
                for i in range(IPN):
                    wait_job(dve, b, "vrep", i)
                    nc.vector.tensor_copy(vip_rep[:, i, :], bank("vrep", i)[:, 0:C]).then_inc(freed["D"], 1)

                run_heads(step1, dve, b)
                dve.wait_ge(out_moved, HEADS * (b + 1) + CREDIT)
                dve.wait_ge(sz_moved, HEADS * (b + 1))
                o1 = out_all[:, 0:nd * OUT1].rearrange("p (n w) -> p n w", w=OUT1)
                szf = sz_all[:, :, :, :].rearrange("p h c w -> p (h c) w")
                rz, n2, rn = stat[:, :, 2:3], stat[:, :, 3:4], stat[:, :, 4:5]
                top, tot = stat[:, :, 5:6], stat[:, :, 6:7]
                link(b, nc.vector.reciprocal(rz, szf[:, :, IPN:IPN + 1]))
                link(b, nc.vector.tensor_tensor(n2, o1[:, :, NA:NA + 1], o1[:, :, NB:NB + 1], ALU.add))
                link(b, nc.vector.tensor_tensor(n2, n2, rz, ALU.mult))
                link(b, nc.vector.tensor_tensor(n2, n2, rz, ALU.mult))
                nc.vector.tensor_scalar_max(root[:, 0:nd], stat[:, :, 3], EPS * EPS)
                nc.vector.tensor_scalar_max(root[:, nd:nd + IPN], ip_norm2[:, :], EPS * EPS).then_inc(ask_root, 1)
                dve.wait_ge(root_in, b + 1)
                nc.vector.reciprocal(rip[:, :], root[:, nd:nd + IPN])
                link(b, nc.vector.reciprocal(stat[:, :, 4], root[:, 0:nd]))
                link(b, nc.vector.tensor_tensor(rn, rn, rz, ALU.mult))
                link(b, nc.vector.tensor_tensor(fused[:, :, :], o1[:, :, A1:A1 + IPN], rn.to_broadcast([P, nd, IPN]), ALU.mult))
                for i in range(IPN):
                    last = nc.vector.tensor_scalar(fused[:, :, i], fused[:, :, i], rip[:, i:i + 1], SEM_SCALE / 2, ALU.mult, ALU.mult)
                link(b, last)
                link(b, nc.vector.scalar_tensor_tensor(out=fused[:, :, :], in0=szf[:, :, 0:IPN], scalar=SCALE, in1=fused[:, :, :],
                                                       op0=ALU.mult, op1=ALU.add))
                link(b, nc.vector.tensor_reduce(out=top, in_=fused[:, :, :], axis=AX.X, op=ALU.max))
                nc.vector.tensor_tensor(fused[:, :, :], fused[:, :, :], top.to_broadcast([P, nd, IPN]), ALU.subtract)\
                    .then_inc(ask_exp, 1)
                nc.vector.tensor_tensor(wide[0], o1[:, :, V1:V1 + D], rz.to_broadcast([P, nd, D]), ALU.mult)
                dve.wait_ge(exp_in, b + 1)
                link(b, nc.vector.tensor_reduce(out=tot, in_=fused[:, :, :], axis=AX.X, op=ALU.add))
                link(b, nc.vector.reciprocal(tot, tot))
                tot3 = stat[:, :, 6].rearrange("p (h c) -> p h c", c=SC)
                mask3 = mask_sb[:, :].unsqueeze(1).to_broadcast([P, HEADS, SC])
                link(b, nc.vector.tensor_tensor(tot3, tot3, mask3, ALU.mult))
                link(b, nc.vector.tensor_tensor(fused[:, :, :], fused[:, :, :], tot.to_broadcast([P, nd, IPN]), ALU.mult))
                f4 = fused[:, :, :].rearrange("p (h c) i -> p h c i", c=SC)
                vr = vip_rep[:, :, :].rearrange("p i (h d) -> p i h d", d=D)
                for i in range(IPN):
                    for c in range(SC):
                        last = nc.vector.tensor_tensor(w4[1][:, :, c, :], f4[:, :, c, i:i + 1].to_broadcast([P, HEADS, D]),
                                                       vr[:, i, :, :], ALU.mult)
                    link(b, last)
                    if i < IPN - 1:
                        link(b, nc.vector.tensor_tensor(wide[0], wide[0], wide[1], ALU.add))
                    if ahead and i > 0:
                        low(b, "k0", i - 1)
                nc.vector.tensor_tensor(by_head, w4[0], w4[1], ALU.add).then_inc(heads_ready, 1)
                if ahead:
                    lows(b, "q0")
                for m in range(CBN):
                    wait_job(dve, b, "y", m)
                    nc.vector.scalar_tensor_tensor(out=x1_sb[0:CB[m], m, :], in0=bank("y", m)[0:CB[m], :],
                                                   scalar=bias_o[1][0:CB[m], m:m + 1], in1=x1_sb[0:CB[m], m, :],
                                                   op0=ALU.add, op1=ALU.add).then_inc(freed["D"], 1)
                assert links[0] <= CHAIN_B, links[0]
                while links[0] < CHAIN_B:
                    link(b, nc.vector.memset(dump[:, 8:9], 0.0))

            lows(FIRST, "k0")
            lows(FIRST, "q0")
            run_batches(dve, batch)

        @block.tensor
        def _(pe):
            pe.wait_ge(built, 2)
            pe.wait_ge(ident_r_in, 1)
            pe.wait_ge(dve_consts_in, 1)
            pe.wait_ge(weights_in, WEIGHTS)

            def mm(out, lhsT, rhs, start, stop):
                return nc.tensor.matmul(out, lhsT, rhs, start=start, stop=stop)

            def free_bank(b, name, m):
                k = JOB[name, m]
                if b is not FIRST and k < RING:
                    for e in "AD":
                        pe.wait_ge(freed[e], freed_value(b, e, 0))
                elif k - RING >= FIRST_NEXT if b is FIRST else not left_out(b, k) or k - RING >= FIRST_NEXT + len(NEXT):
                    wait_freed(pe, b, *JOBS[k - RING][0:2])
                return bank(name, m)

            def over_e(out, lhs, rhs):
                for e in range(EB):
                    last = mm(out, lhs(e), rhs(e), e == 0, e == EB - 1)
                return last

            def over_c(out, w, m, src):
                for e in range(CBN):
                    last = mm(out, w[0:CB[e], e, m * P:m * P + CB[m]], src[0:CB[e], e, :], e == 0, e == CBN - 1)
                return last

            def head_scores(b, l, n, k, turn, half):
                g = HEADS * b + n
                slot = (k + 2) % SLOTS
                if half == 0:
                    pe.wait_ge(slots_in[l][slot], SLOT_LOADS * (TURNS * b + turn + (k + 2) // SLOTS + 1))
                if l == 0:
                    pe.wait_ge(max_half[0], 2 * (g + 2) + half + CREDIT)
                else:
                    pe.wait_ge(p_chunk, SC * (g + 2) + 2 * half + CREDIT)
                for i in range(2):
                    c = 2 * half + i
                    last = mm(ps_s[:, i, :], q_slot[slot][0:SCORE_ROWS, P * c:P * c + P], k_slot[slot][0:SCORE_ROWS, :], True, True)
                last.then_inc(s_half[l], 1)

            def head_maxT(b, l, n, par):
                pe.wait_ge(max_half[l], 2 * (HEADS * b + n + 2) + CREDIT)
                for c in range(SC):
                    rows = row_max[l][1 - par][:, c, :]
                    last = mm(ps_m[0:SHIFT_ROWS, P * c:P * c + P], rows if l == 0 else rows.to_broadcast([P, SHIFT_ROWS]),
                              ident_r[:, :], True, True)
                last.then_inc(maxT_done[l], 1)

            def head_scoresT(b, l, n, k, half):
                g, slot = HEADS * b + n, (k + 1) % SLOTS
                if half == 0:
                    pe.wait_ge(shift_in[l], g + 2)
                pe.wait_ge(pt_half[l], 2 * (g + 1) + half + CREDIT)
                for i in range(2):
                    t = 2 * half + i
                    last = mm(ps_t[:, i, :], k_slot[slot][:, P * t:P * t + P], q_slot[slot][:, :], True, True)
                last.then_inc(st_half[l], 1)

            def step0(b, n, k, turn, use, transposed, scores):
                par = k % 2
                g = HEADS * b + n

                def values(t):
                    last = mm(ps_w[par][0:V0W, :], v0_slot[par][:, t, :], probsT[par][:, t, :], t == 0, t == TB - 1)
                    if t == TB - 1:
                        last.then_inc(oT_done, 1)

                if use:
                    pe.wait_ge(pt_half[0], 2 * g + 1 + CREDIT)
                    pe.wait_ge(oT_moved, g - 1 + CREDIT)
                    pe.wait_ge(v0_in, g + 1)
                    values(0)
                if transposed:
                    head_maxT(b, 0, n, par)
                if use:
                    values(1)
                if transposed:
                    head_scoresT(b, 0, n, k, 0)
                if scores:
                    head_scores(b, 0, n, k, turn, 0)
                if use:
                    pe.wait_ge(pt_half[0], 2 * g + 2 + CREDIT)
                    values(2)
                    values(3)
                if transposed:
                    head_scoresT(b, 0, n, k, 1)
                if scores:
                    head_scores(b, 0, n, k, turn, 1)
                if use:
                    pe.wait_ge(oT_moved, g + 1 + CREDIT)
                    pe.wait_ge(o_moved, g + CREDIT)
                    pe.sem_inc(passed, 1)
                    for c in range(SC):
                        last = nc.tensor.transpose(ps_b[:, V0W * c:V0W * c + V0W], outT0[par][:, P * c:P * c + P],
                                                   ident[0:V0W, 0:V0W])
                    last.then_inc(o_done, 1)

            def step1(b, n, k, turn, use, transposed, scores):
                par = k % 2
                g = HEADS * b + n

                def gram_product(c):
                    pe.wait_ge(z_done, SC * g + c - 1 + CREDIT)
                    out = ps_w[c % 2]
                    for t in range(TB):
                        rows = P if t < TB - 1 else P - IPN
                        lo = P * max(t, 1) - P
                        last = mm(out[:, lo:GW], probsT[par][0:rows, t, P * c:P * c + P], gram[par][0:rows, t, lo:GW],
                                  t == 0, t == TB - 1)
                    last.then_inc(w_done, 1)

                if transposed:
                    head_maxT(b, 1, n, par)
                if use:
                    pe.wait_ge(pt_half[1], 2 * g + 1 + CREDIT)
                    pe.wait_ge(zb_done, g + CREDIT)
                    for c in range(SC):
                        last = mm(ps_b[:, P * c:P * c + P], probsT[par][:, 0, P * c:P * c + P], gram00[:, :], True, True)
                    last.then_inc(b_done, 1)
                    pe.wait_ge(pt_half[1], 2 * g + 2 + CREDIT)
                    pe.wait_ge(v_in, g + 1)
                    gram_product(0)
                if transposed:
                    head_scoresT(b, 1, n, k, 0)
                if scores:
                    head_scores(b, 1, n, k, turn, 0)
                if use:
                    gram_product(1)
                if transposed:
                    head_scoresT(b, 1, n, k, 1)
                if use:
                    gram_product(2)
                if scores:
                    head_scores(b, 1, n, k, turn, 1)
                if use:
                    gram_product(3)

            def keys(b, name, split, text):
                for m in range(CBN):
                    out, cols = free_bank(b, name, m), slice(m * P, m * P + CB[m])
                    over_e(out[0:CB[m], 0:text], lambda e: w_big[name][:, e, cols], lambda e: ctx_sb[:, e, 0:text])
                    over_e(out[0:CB[m], text:T], lambda e: w_big[split][:, e, cols], lambda e: ctx_sb[:, e, text:T])\
                        .then_inc(job_done, 1)

            def by_channels(b, name, w, src):
                for m in range(CBN):
                    over_c(free_bank(b, name, m)[0:CB[m], :], w_small[w], m, src).then_inc(job_done, 1)

            def by_keys(b, name, w):
                for t in range(TB):
                    over_e(free_bank(b, name, t)[:, 0:C], lambda e: ctx_sb[:, e, P * t:P * t + P],
                           lambda e: w_big[w][:, e, :]).then_inc(job_done, 1)

            def for_layer0(b, batch):
                pe.wait_ge(ctx_in, 16 * batch + 16)
                pe.wait_ge(x_in, 32 * batch + 32)
                over_e(free_bank(b, "v0t", 0)[0:TEXT0, 0:C], lambda e: ctx_sb[:, e, 0:TEXT0],
                       lambda e: w_big["v0"][:, e, :]).then_inc(job_done, 1)
                by_keys(b, "v0i", "vi0")
                keys(b, "k0", "ki0", TEXT0)
                by_channels(b, "q0", "q0", x_sb)

            def transposed_heads(b, name, l):
                pe.wait_ge(heads_ready, 2 * b + l + 1)
                for m in range(CBN):
                    out = free_bank(b, name, m)
                    pe.sem_inc(passed, 1)
                    for c in range(SC):
                        last = nc.tensor.transpose(out[0:CB[m], P * c:P * c + P], heads_out[:, c, P * m:P * m + CB[m]],
                                                   ident[:, :])
                    last.then_inc(job_done, 1)
                wait_freed(pe, b, name, CBN - 1)

            def batch(b, ahead):
                run_heads(step0, pe, b)
                keys(b, "k1", "ki1", TEXT1)
                for i in range(TB):
                    over_e(free_bank(b, "g", i)[:, 0:T - P * i], lambda e: ctx_sb[:, e, P * i:P * i + P],
                           lambda e: ctx_sb[:, e, P * i:T]).then_inc(job_done, 1)
                transposed_heads(b, "tr0", 0)
                by_channels(b, "x1", "o0", heads_outT)
                wait_freed(pe, b, "x1", CBN - 1)
                by_channels(b, "q1", "q1", x1_sb)
                by_keys(b, "v1", "v1")
                pe.wait_ge(ip_sq_in, b + 1)
                over_e(free_bank(b, "ipn", 0)[:, 0:IPN], lambda e: ones[:, :], lambda e: ip_sq[:, e, :]).then_inc(job_done, 1)
                over_e(free_bank(b, "vip", 0)[0:IPN, 0:C], lambda e: ctx_sb[:, e, TEXT1:T], lambda e: w_big["vi1"][:, e, :])\
                    .then_inc(job_done, 1)
                wait_freed(pe, b, "vip", 0)
                for i in range(IPN):
                    mm(free_bank(b, "vrep", i)[:, 0:C], pick[:, i, :], vip[:, :], True, True).then_inc(job_done, 1)
                wait_freed(pe, b, "vrep", IPN - 1)
                pe.wait_ge(gram_copied, b + 1)
                run_heads(step1, pe, b)
                if ahead:
                    for_layer0(b, b + 1)
                transposed_heads(b, "tr1", 1)
                by_channels(b, "y", "o1", heads_outT)
                if ahead:
                    wait_freed(pe, b, "y", CBN - 1)

            for_layer0(FIRST, 0)
            wait_freed(pe, FIRST, "q0", CBN - 1)
            run_batches(pe, batch)


def kernel(x, ctx_2048, fside_S_0, L0_xattn_Wq, L0_xattn_Wk, L0_xattn_Wv, L0_xattn_Wk_ip, L0_xattn_Wv_ip, L0_xattn_Wo,
           L0_xattn_bo, L1_xattn_W_q, L1_xattn_W_k, L1_xattn_W_v, L1_xattn_W_k_ip, L1_xattn_W_v_ip, L1_xattn_W_out,
           L1_xattn_b_out):
    import numpy as np
    import concourse.bacc as bacc
    from concourse.bass_utils import run_bass_kernel_spmd

    given = {
        "xT": np.asarray(x).transpose(0, 2, 1),
        "ctxT": np.asarray(ctx_2048).transpose(0, 2, 1),
        "mask": np.asarray(fside_S_0).reshape(SC, P).T,
        "wq0": np.asarray(L0_xattn_Wq).T,
        "wk0": np.asarray(L0_xattn_Wk).T,
        "wv0": np.asarray(L0_xattn_Wv).T,
        "wki0": np.asarray(L0_xattn_Wk_ip).T,
        "wvi0": np.asarray(L0_xattn_Wv_ip).T,
        "wo0": np.asarray(L0_xattn_Wo).T,
        "bo0": np.asarray(L0_xattn_bo).reshape(C, 1),
        "wq1": np.asarray(L1_xattn_W_q),
        "wk1": np.asarray(L1_xattn_W_k),
        "wv1": np.asarray(L1_xattn_W_v),
        "wki1": np.asarray(L1_xattn_W_k_ip),
        "wvi1": np.asarray(L1_xattn_W_v_ip),
        "wo1": np.asarray(L1_xattn_W_out),
        "bo1": np.asarray(L1_xattn_b_out).reshape(C, 1),
    }
    nc = bacc.Bacc("TRN2", target_bir_lowering=False, num_devices=1)
    arrays, args = {}, []
    for name, a in given.items():
        a = np.ascontiguousarray(a)
        arrays[f"in_{name}"] = a
        args.append(nc.dram_tensor(f"in_{name}", a.shape, mybir.dt.from_np(a.dtype), kind="ExternalInput").ap())
    out = nc.dram_tensor("outT", [BATCH, C, S], F32, kind="ExternalOutput").ap()
    build(nc, *args, out)
    r = run_bass_kernel_spmd(nc, [arrays], core_ids=[0])
    return np.ascontiguousarray(r.results[0]["outT"].transpose(0, 2, 1))
```

```python
from contextlib import ExitStack

import concourse.bass as bass
from concourse import mybir

ACT = mybir.ActivationFunctionType
ALU = mybir.AluOpType
AX = mybir.AxisListType
F32 = mybir.dt.float32
F32R = mybir.dt.float32r

P = 128
BATCH, S, C, E, T = 4, 512, 320, 512, 512
HEADS, D = 20, 16

TEXT0 = 77
IPN = 4
TEXT1 = T - IPN
SCALE = float(D) ** -0.5
SEM_SCALE = 0.5
EPS = 1e-12
SC = S // P
TB = T // P
EB = E // P
CB = [P, P, C - 2 * P]
CBN = len(CB)


PART = D
SCORE_ROWS = 3 * PART
SHIFT_ROW = 64
SHIFT_ROWS = 33
ALL_ROWS = SHIFT_ROW + SHIFT_ROWS
SLOTS = 4
TURNS = HEADS // SLOTS
SLOT_LOADS = 2 * 16
ROW_PARTS = {"q": (0, 0, 1), "k": (0, 1, 0)}
STORES = 2 * 3 * 16

V0W = 2 * (D + 1)
V0S = 2 * V0W
GA = T - P
GV = GA + D
GW = GV + D
GN = TEXT1 - P
OUT1 = IPN + D + 4
A1, V1, NA, NB = 0, IPN, IPN + D, IPN + D + 1
HO = IPN + 2 * D
SZW = IPN + 1

NEXT = (
    [("k0", m, "D") for m in range(CBN)]
    + [("q0", m, "D") for m in range(CBN)]
    + [("v0t", 0, "A")]
    + [("v0i", t, "A") for t in range(TB)]
)
JOBS = (
    [("k1", m, "D") for m in range(CBN)]
    + [("tr0", m, "A") for m in range(CBN)]
    + [("x1", m, "D") for m in range(CBN)]
    + [("q1", m, "D") for m in range(CBN)]
    + [("g", i, "D") for i in range(TB)]
    + [("v1", t, "A") for t in range(TB)]
    + [("ipn", 0, "D"), ("vip", 0, "D")]
    + [("vrep", n, "D") for n in range(IPN)]
    + NEXT
    + [("tr1", m, "A") for m in range(CBN)]
    + [("y", m, "D") for m in range(CBN)]
)
JOB = {(name, m): k for k, (name, m, _) in enumerate(JOBS)}
FIRST_NEXT = JOB["k0", 0]
FREED_BY = [e for _, _, e in JOBS]
BEFORE = {e: [x for _, _, x in NEXT].count(e) for e in "AD"}
PER_B = {e: FREED_BY.count(e) for e in "AD"}
HIGHS = ("k1", "q1", "k0", "q0")
FIRST = "first"
RING = 4
WEIGHTS = 16 * (4 + 6 + 2 * CBN + 1)
CREDIT = 8
CREDIT1 = 2 * CREDIT


def build(nc, xT, ctxT, mask, wq0, wk0, wv0, wki0, wvi0, wo0, bo0, wq1, wk1, wv1, wki1, wvi1, wo1, bo1, outT):
    with ExitStack() as ctx:
        def sb(name, shape, dt=F32):
            return ctx.enter_context(nc.sbuf_tensor(name, shape, dt))

        def sem(name):
            return ctx.enter_context(nc.semaphore(name))

        scratch = {n: nc.dram_tensor(f"parts_{n}", [3, HEADS, D, S], F32, kind="Internal").ap()
                   for n in ("k0", "q0", "k1", "q1")}

        w_small = {n: sb(f"w_{n}", [P, CBN, C]) for n in ("q0", "o0", "q1", "o1")}
        w_big = {n: sb(f"w_{n}", [P, EB, C]) for n in ("k0", "v0", "ki0", "vi0", "k1", "v1", "ki1", "vi1")}
        bias_o = [sb(f"bias_o{l}", [P, CBN]) for l in range(2)]
        mask_sb = sb("mask_sb", [P, SC])
        ctx_sb = sb("ctx_sb", [P, EB, T])
        x_sb = sb("x_sb", [P, CBN, S])
        x1_sb = sb("x1_sb", [P, CBN, S])
        ident = sb("ident", [P, P])
        ident_r = sb("ident_r", [P, P], F32R)
        ones = sb("ones", [P, 1])
        ip_rows = sb("ip_rows", [P, 1])
        v0_sb = sb("v0_sb", [P, 1 + TB, HEADS, D])
        v1_sb = sb("v1_sb", [P, TB, C])
        gram00 = sb("gram00", [P, P])
        gram = [sb(f"gram{p}", [P, TB, GW], F32R) for p in range(2)]
        gram_low = sb("gram_low", [P, TB, GA], F32R)
        ip_sq = sb("ip_sq", [P, EB, IPN])
        v0_slot = [sb(f"v0_slot{p}", [P, TB, V0S], F32R) for p in range(2)]
        vip = sb("vip", [IPN, C])
        vip_rep = sb("vip_rep", [P, IPN, C])
        q_slot = [sb(f"q_slot{i}", [ALL_ROWS, S], F32R) for i in range(SLOTS)]
        k_slot = [sb(f"k_slot{i}", [ALL_ROWS, T], F32R) for i in range(SLOTS)]
        row_max = [[sb(f"row_max{l}{p}", [P, SC, SHIFT_ROWS if l == 0 else 1], F32R) for p in range(2)] for l in range(2)]
        probsT = sb("probsT", [P, TB, S])
        probsT_high = [sb(f"probsT_high{p}", [P, TB, S], F32R) for p in range(2)]
        probsT_low = [sb(f"probsT_low{p}", [P, TB, S], F32R) for p in range(2)]
        probs = [sb(f"probs{p}", [P, SC, S]) for p in range(2)]
        exp_bias = [sb(f"exp_bias{p}", [P, SC]) for p in range(2)]
        sz = [sb(f"sz{p}", [P, SC, SZW]) for p in range(2)]
        head_out = [sb(f"head_out{p}", [P, SC, HO + 2]) for p in range(2)]
        out_all = sb("out_all", [P, HEADS * SC * V0W])
        o0_all = out_all[:, :].rearrange("p (h c w) -> p h c w", h=HEADS, c=SC)
        o1_all = out_all[:, 0:HEADS * SC * OUT1].rearrange("p (h c w) -> p h c w", h=HEADS, c=SC)
        sz_all = sb("sz_all", [P, HEADS, SC, SZW])
        dump = sb("dump", [P, 16])
        heads_out = probsT[:, :, 0:C]
        heads_outT = probs[0][:, 0:CBN, :]
        outT0 = [probs[0][0:V0S, p, :] for p in range(2)]
        nd = HEADS * SC
        stat = sb("stat", [P, nd, 8])
        root = sb("root", [P, nd + IPN])
        ip_norm2 = sb("ip_norm2", [P, IPN])
        rip = sb("rip", [P, IPN])
        fused = sb("fused", [P, nd, IPN])
        wide = [probs[i][:, :, :].rearrange("p c s -> p (c s)")[:, 0:nd * D].rearrange("p (n d) -> p n d", d=D)
                for i in range(2)]
        halves = {"k": [t[:, 0:CBN, :] for t in probsT_high], "q": [t[:, 0:CBN, :] for t in probsT_low]}
        parts = {n: halves[n[0]] for n in scratch}

        ps_s = ctx.enter_context(nc.psum_tensor("ps_s", [P, 2, 512], F32))
        ps_t = ctx.enter_context(nc.psum_tensor("ps_t", [P, 2, 512], F32))
        ps_w = [ctx.enter_context(nc.psum_tensor(f"ps_w{i}", [P, 512], F32)) for i in range(2)]
        ps_b = ctx.enter_context(nc.psum_tensor("ps_b", [P, 512], F32))
        ps_m = ctx.enter_context(nc.psum_tensor("ps_m", [P, 512], F32))
        ring = [ps_s[:, 0, :], ps_s[:, 1, :], ps_t[:, 0, :], ps_t[:, 1, :]]
        late = {("ipn", 0): ps_b[:, :], ("vip", 0): ps_w[0][:, :]}
        late.update({("vrep", i): ps_w[i % 2][:, :] for i in range(IPN)})

        weights0_in = {n: sem(f"weights0_in_{n}") for n in "kqv"}
        weights_in = sem("weights_in")
        filled, built = sem("filled"), sem("built")
        ident_r_in = sem("ident_r_in")
        dve_consts_in = sem("dve_consts_in")
        ctx_in, x_in = sem("ctx_in"), sem("x_in")
        job_done = sem("job_done")
        freed = {"A": sem("freed_by_act"), "D": sem("freed_by_dve")}
        high_in = sem("high_in")
        ip_sq_in = sem("ip_sq_in")
        gram_copied = sem("gram_copied")
        stored = {n: sem(f"stored_{n}") for n in scratch}
        y_out = sem("y_out")
        passed = sem("passed")
        heads_ready = sem("heads_ready")
        chain = sem("chain")
        ask_root, ask_exp = sem("ask_root"), sem("ask_exp")
        root_in, exp_in = sem("root_in"), sem("exp_in")
        slots_in = [[sem(f"slots_in{l}{i}") for i in range(SLOTS)] for l in range(2)]
        s_half = sem("s_half")
        max_half = sem("max_half")
        s_chunk = sem("s_chunk")
        max_chunk = sem("max_chunk")
        bias_in = sem("bias_in")
        p_chunk = sem("p_chunk")
        st_block = [sem(f"st_block{l}") for l in range(2)]
        pt_block = [sem(f"pt_block{l}") for l in range(2)]
        low_block = [sem(f"low_block{l}") for l in range(2)]
        low_last = sem("low_last")
        maxT_done = [sem(f"maxT_done{l}") for l in range(2)]
        shift_in = [sem(f"shift_in{l}") for l in range(2)]
        gram_high = sem("gram_high")
        v0_high, v_high = sem("v0_high"), sem("v_high")
        v0_in = sem("v0_in")
        oT_done = sem("oT_done")
        oT_moved = sem("oT_moved")
        o_done = sem("o_done")
        o_moved = sem("o_moved")
        v_in = sem("v_in")
        b_done, w_done = sem("b_done"), sem("w_done")
        zb_done, z_done = sem("zb_done"), sem("z_done")
        sz_moved, out_moved = sem("sz_moved"), sem("out_moved")

        def left_out(b, k):
            return b == BATCH - 1 if isinstance(b, int) and k > FIRST_NEXT else False

        def jobs_done(b, k):
            if b is FIRST:
                return k - FIRST_NEXT
            return len(JOBS) * b + k + (0 if left_out(b, k) else len(NEXT))

        def freed_value(b, e, k):
            if b is FIRST:
                return CREDIT + FREED_BY[FIRST_NEXT:k].count(e)
            return PER_B[e] * b + CREDIT + FREED_BY[:k].count(e) + (0 if left_out(b, k) else BEFORE[e])

        def wait_freed(eng, b, name, m):
            k = JOB[name, m]
            e = FREED_BY[k]
            eng.wait_ge(freed[e], freed_value(b, e, k + 1))

        def wait_job(eng, b, name, m):
            eng.wait_ge(job_done, jobs_done(b, JOB[name, m] + 1))

        def bank(name, m):
            return late[name, m] if (name, m) in late else ring[JOB[name, m] % RING]

        def run_batches(eng, batch):
            with eng.Fori(0, BATCH - 1) as b:
                batch(b, True)
            batch(BATCH - 1, False)

        def run_heads(step, eng, b, after_first=None):
            step(b, -2, SLOTS - 2, -1, False, False, True)
            step(b, -1, SLOTS - 1, -1, False, True, True)
            if after_first:
                after_first()
            with eng.Fori(0, TURNS - 1) as turn:
                for k in range(SLOTS):
                    step(b, SLOTS * turn + k, k, turn, True, True, True)
            for k in range(SLOTS):
                step(b, HEADS - SLOTS + k, k, TURNS - 1, True, k < SLOTS - 1, k < SLOTS - 2)

        def load_ctx(eng, batch):
            eng.dma_start(ctx_sb[:, :, :], ctxT[batch, :, :].rearrange("(k p) t -> p k t", p=P)).then_inc(ctx_in, 16)

        def load_x(eng, batch):
            eng.dma_start(x_sb[:, 0:2, :], xT[batch, 0:2 * P, :].rearrange("(k p) s -> p k s", p=P)).then_inc(x_in, 16)
            eng.dma_start(x_sb[0:CB[2], 2, :], xT[batch, 2 * P:C, :]).then_inc(x_in, 16)

        block = ctx.enter_context(nc.Block())

        @block.sync
        def _(sp):
            def load_big(n, src, there):
                sp.dma_start(w_big[n][:, :, :], src.rearrange("(k p) n -> p k n", p=P)).then_inc(there, 16)

            def load_small(n, src, there):
                sp.dma_start(w_small[n][:, 0:2, :], src[0:2 * P, :].rearrange("(k p) n -> p k n", p=P)).then_inc(there, 16)
                sp.dma_start(w_small[n][0:CB[2], 2, :], src[2 * P:C, :]).then_inc(there, 16)

            load_ctx(sp, 0)
            load_big("k0", wk0, weights0_in["k"])
            load_big("ki0", wki0, weights0_in["k"])
            load_x(sp, 0)
            load_small("q0", wq0, weights0_in["q"])
            load_big("v0", wv0, weights0_in["v"])
            load_big("vi0", wvi0, weights0_in["v"])
            for n, src in (("k1", wk1), ("ki1", wki1), ("v1", wv1), ("vi1", wvi1)):
                load_big(n, src, weights_in)
            for n, src in (("o0", wo0), ("q1", wq1), ("o1", wo1)):
                load_small(n, src, weights_in)
            for l, src in ((0, bo0), (1, bo1)):
                for m in range(CBN):
                    sp.dma_start(bias_o[l][0:CB[m], m:m + 1], src[m * P:m * P + CB[m], :]).then_inc(weights_in, 16)
            sp.dma_start(mask_sb[:, :], mask).then_inc(weights_in, 16)

            def store(b, name):
                for i, part in enumerate(ROW_PARTS[name[0]]):
                    dst = scratch[name][i, :, :, :].rearrange("h d s -> (h d) s")
                    src = parts[name][part].bitcast(F32)
                    sp.dma_start(dst[0:2 * P, :].rearrange("(k p) s -> p k s", p=P), src[:, 0:2, :]).then_inc(stored[name], 16)
                    sp.dma_start(dst[2 * P:C, :], src[0:CB[2], 2, :]).then_inc(stored[name], 16)

            def load_slots(b, l, n, k):
                used = HEADS * b + n - SLOTS + 1
                sp.wait_ge(pt_block[l], TB * used + CREDIT1)
                for slot, src in ((q_slot[k], scratch[f"q{l}"]), (k_slot[k], scratch[f"k{l}"])):
                    sp.dma_start(slot[0:SCORE_ROWS, :].bitcast(F32), src[:, n, :, :])\
                        .then_inc(slots_in[l][k], 16)

            def load_all(b, l):
                with sp.Fori(0, TURNS) as turn:
                    for k in range(SLOTS):
                        load_slots(b, l, SLOTS * turn + k, k)

            def split_and_loaded(b, batch, l, names):
                for name in names:
                    wait_freed(sp, b, name, CBN - 1)
                    store(b, name)
                for name in names:
                    sp.wait_ge(stored[name], STORES * (batch + 1))
                sp.sem_inc(passed, 1)
                load_all(batch, l)

            split_and_loaded(FIRST, 0, 0, ("k0", "q0"))
            with sp.Fori(0, BATCH - 1) as b:
                split_and_loaded(b, b, 1, ("k1", "q1"))
                split_and_loaded(b, b + 1, 0, ("k0", "q0"))
            split_and_loaded(BATCH - 1, BATCH - 1, 1, ("k1", "q1"))

        @block.gpsimd
        def _(pool):
            nc.gpsimd.memset(ident[:, :], 0.0).then_inc(filled, 1)
            nc.gpsimd.memset(ones[:, :], 1.0).then_inc(filled, 1)
            nc.gpsimd.memset(out_all[:, 0:1], 0.0).then_inc(out_moved, CREDIT)
            nc.gpsimd.memset(out_all[:, 1:2], 0.0).then_inc(low_last, CREDIT)
            pool.wait_ge(filled, 2)
            nc.gpsimd.affine_select(out=ident[:, :], in_=ident[:, :], compare_op=ALU.not_equal, fill=1.0, base=0,
                                    pattern=[[-1, P]], channel_multiplier=1).then_inc(built, 1)

            def step0(b, n, k, turn, use, transposed, scores):
                par = k % 2
                if scores:
                    pool.wait_ge(oT_moved, HEADS * b + n + 1 + CREDIT) if use else None
                    pool.sem_inc(passed, 1)
                    pieces = [(slice(0, 1), slice(0, D), v0_sb[:, 0:1, n + 2, :]),
                              (slice(0, TB), slice(D + 1, 2 * D + 1), v0_sb[:, 1:1 + TB, n + 2, :])]
                    for blocks, cols, src in pieces:
                        last = nc.gpsimd.tensor_copy(v0_slot[par][:, blocks, cols], src)
                    last.then_inc(v0_high, 1)
                    pool.wait_ge(v0_high, HEADS * b + n + 3)
                    pool.sem_inc(passed, 1)
                    for blocks, cols, src in pieces:
                        low = slice(cols.start + V0W, cols.stop + V0W)
                        last = nc.gpsimd.tensor_tensor(v0_slot[par][:, blocks, low], src, v0_slot[par][:, blocks, cols].bitcast(F32),
                                                       ALU.subtract)
                    last.then_inc(v0_in, 1)
                if transposed:
                    pool.wait_ge(pt_block[0], TB * (HEADS * b + n + 1) + TB + CREDIT1)
                    nc.gpsimd.tensor_tensor(probsT_low[1 - par][:, TB - 1, :], probsT[:, TB - 1, :],
                                            probsT_high[1 - par][:, TB - 1, :].bitcast(F32), ALU.subtract).then_inc(low_last, 1)

            def step1(b, n, k, turn, use, transposed, scores):
                par = k % 2
                g = HEADS * b + n
                if scores:
                    for c in range(SC):
                        pool.wait_ge(max_chunk, SC * (g + 2) + c + 1 + CREDIT)
                        pool.sem_inc(passed, 1)
                        nc.gpsimd.tensor_scalar_mul(exp_bias[par][:, c:c + 1], row_max[1][par][:, c, 0:1].bitcast(F32), -SCALE)\
                            .then_inc(bias_in, 1)
                if use:
                    pool.wait_ge(z_done, SC * (g + 1) + CREDIT)
                    pool.sem_inc(passed, 1)
                    ho = head_out[par]
                    nc.gpsimd.tensor_copy(o1_all[:, n, :, A1:A1 + IPN], ho[:, :, 0:IPN])
                    nc.gpsimd.tensor_copy(o1_all[:, n, :, NA:NB + 1], ho[:, :, HO:HO + 2])
                    nc.gpsimd.tensor_tensor(o1_all[:, n, :, V1:V1 + D], ho[:, :, IPN:IPN + D], ho[:, :, IPN + D:HO], ALU.add)\
                        .then_inc(out_moved, 1)
                if scores:
                    src = v1_sb[:, :, :].rearrange("p t (h d) -> p t h d", d=D)[:, :, n + 2, :]
                    nc.gpsimd.tensor_copy(gram[par][:, :, GA:GV], src).then_inc(v_high, 1)
                    pool.wait_ge(v_high, HEADS * b + n + 3)
                    pool.sem_inc(passed, 1)
                    nc.gpsimd.tensor_tensor(gram[par][:, :, GV:GW], src, gram[par][:, :, GA:GV].bitcast(F32), ALU.subtract)\
                        .then_inc(v_in, 1)
                    pool.wait_ge(p_chunk, SC * (g + 3) + CREDIT)
                    pool.sem_inc(passed, 1)
                    nc.gpsimd.tensor_copy(sz_all[:, n + 2, :, 0:IPN + 1], sz[par][:, :, 0:IPN + 1]).then_inc(sz_moved, 1)

            wait_freed(pool, FIRST, "v0i", TB - 1)
            pool.sem_inc(passed, 1)

            def batch(b, ahead):
                run_heads(step0, pool, b)
                wait_freed(pool, b, "g", TB - 1)
                pool.sem_inc(passed, 1)
                for i in range(TB):
                    lo = P * max(i, 1) - P
                    last = nc.gpsimd.tensor_copy(gram[1][:, i, lo:GA], gram[0][:, i, lo:GA])
                last.then_inc(gram_copied, 1)
                wait_freed(pool, b, "v1", TB - 1)
                pool.sem_inc(passed, 1)
                run_heads(step1, pool, b)
                if ahead:
                    wait_freed(pool, b, "v0i", TB - 1)
                    pool.sem_inc(passed, 1)

            run_batches(pool, batch)

        @block.scalar
        def _(act):
            act.wait_ge(built, 1)
            nc.scalar.activation(ident_r[:, :], ident[:, :], ACT.Copy).then_inc(ident_r_in, 1)
            for i, s in enumerate((freed["A"], oT_moved, p_chunk, pt_block[0], pt_block[1])):
                nc.scalar.activation(dump[:, i:i + 1], ident[:, 0:1], ACT.Copy).then_inc(s, CREDIT1 if s in pt_block else CREDIT)
            act.wait_ge(dve_consts_in, 1)

            def high(b, name, m):
                wait_job(act, b, name, m)
                nc.scalar.activation(parts[name][0][0:CB[m], m, :], bank(name, m)[0:CB[m], :],
                                     ACT.Copy).then_inc(high_in, 1)

            def shift(b, l, n, k):
                act.wait_ge(maxT_done[l], HEADS * b + n + 2)
                nc.scalar.activation(q_slot[(k + 1) % SLOTS][SHIFT_ROW:ALL_ROWS, :], ps_m[0:SHIFT_ROWS, :], ACT.Copy)\
                    .then_inc(shift_in[l], 1)

            def expT(b, l, n, par, t):
                g = HEADS * b + n
                act.wait_ge(st_block[l], TB * (g + 1) + t + 1)
                nc.scalar.activation(probsT_high[1 - par][:, t, :], ps_t[:, t % 2, :], ACT.Exp, scale=SCALE)
                if l == 1:
                    act.wait_ge(low_block[1], TB * g + t + 1 + CREDIT)
                elif t < TB - 1:
                    act.wait_ge(low_block[0], (TB - 1) * g + t + 1 + CREDIT)
                else:
                    act.wait_ge(low_last, g + 1 + CREDIT)
                nc.scalar.activation(probsT[:, t, :], ps_t[:, t % 2, :], ACT.Exp, scale=SCALE).then_inc(pt_block[l], 1)

            def step0(b, n, k, turn, use, transposed, scores):
                par = k % 2
                if transposed:
                    expT(b, 0, n, par, 0)
                    expT(b, 0, n, par, 1)
                if use:
                    act.wait_ge(oT_done, HEADS * b + n + 1)
                    nc.scalar.activation(outT0[par], ps_w[par][0:V0S, :], ACT.Copy).then_inc(oT_moved, 1)
                if transposed:
                    expT(b, 0, n, par, 2)
                if scores:
                    shift(b, 0, n + 1, k + 1)
                if transposed:
                    expT(b, 0, n, par, 3)

            def step1(b, n, k, turn, use, transposed, scores):
                par = k % 2
                g = HEADS * b + n

                def exps(c):
                    act.wait_ge(z_done, SC * g + c + 1 + CREDIT) if use else None
                    act.wait_ge(bias_in, SC * (g + 2) + c + 1)
                    nc.scalar.activation(probs[par][:, c, 0:TEXT1], ps_s[:, c % 2, 0:TEXT1], ACT.Exp,
                                         bias=exp_bias[par][:, c:c + 1], scale=SCALE,
                                         accum_out=sz[par][:, c, IPN:IPN + 1]).then_inc(p_chunk, 1)

                if transposed:
                    shift(b, 1, n, k)
                for c in range(SC):
                    if transposed:
                        expT(b, 1, n, par, c)
                    if scores and c < 2:
                        exps(c)
                if scores:
                    exps(2)
                    exps(3)

            def v0_text(b):
                wait_job(act, b, "v0t", 0)
                nc.scalar.activation(v0_sb[0:TEXT0, 0, :, :],
                                     bank("v0t", 0)[0:TEXT0, 0:C].rearrange("p (h d) -> p h d", d=D),
                                     ACT.Copy).then_inc(freed["A"], 1)

            def v0_ip(b, t):
                wait_job(act, b, "v0i", t)
                nc.scalar.activation(v0_sb[:, 1 + t, :, :],
                                     bank("v0i", t)[:, 0:C].rearrange("p (h d) -> p h d", d=D),
                                     ACT.Copy, scale=ip_rows[:, :] if t == 0 else 1.0).then_inc(freed["A"], 1)

            def gram_rows(b, i):
                wait_job(act, b, "g", i)
                src = bank("g", i)
                diag = P if i < TB - 1 else P - IPN
                dst = gram00[:, :] if i == 0 else gram[0][:, i, P * (i - 1):P * (i - 1) + diag]
                nc.scalar.activation(dst, src[:, 0:diag], ACT.Copy)
                nc.scalar.activation(gram[0][:, i, P * i - P + diag:GA], src[:, diag:T - P * i], ACT.Copy, scale=2.0)\
                    .then_inc(gram_high, 1)

            def move_transposed(b, name):
                for m in range(CBN):
                    wait_job(act, b, name, m)
                    nc.scalar.activation(heads_outT[0:CB[m], m, :], bank(name, m)[0:CB[m], :], ACT.Copy).then_inc(freed["A"], 1)

            def highs(b, name):
                for m in range(CBN):
                    high(b, name, m)

            def batch(b, ahead):
                run_heads(step0, act, b)
                highs(b, "k1")
                move_transposed(b, "tr0")
                highs(b, "q1")
                for i in range(TB):
                    gram_rows(b, i)
                for t in range(TB):
                    wait_job(act, b, "v1", t)
                    nc.scalar.activation(v1_sb[:, t, :], bank("v1", t)[:, 0:C], ACT.Copy).then_inc(freed["A"], 1)

                def next_inputs():
                    wait_freed(act, b, "vip", 0)
                    load_ctx(act, b + 1)
                    load_x(act, b + 1)

                run_heads(step1, act, b, next_inputs if ahead else None)
                if ahead:
                    high(b, "k0", 0)
                act.wait_ge(ask_root, b + 1)
                nc.scalar.activation(root[:, :], root[:, :], ACT.Sqrt).then_inc(root_in, 1)
                if ahead:
                    high(b, "k0", 1)
                    high(b, "k0", 2)
                act.wait_ge(ask_exp, b + 1)
                nc.scalar.activation(fused[:, :, :], fused[:, :, :], ACT.Exp).then_inc(exp_in, 1)
                if ahead:
                    highs(b, "q0")
                    v0_text(b)
                    for t in range(TB):
                        v0_ip(b, t)
                move_transposed(b, "tr1")
                for m in range(CBN):
                    wait_freed(act, b, "y", m)
                    act.dma_start(outT[b, m * P:m * P + CB[m], :], x1_sb[0:CB[m], m, :]).then_inc(y_out, 16)

            highs(FIRST, "k0")
            highs(FIRST, "q0")
            v0_text(FIRST)
            for t in range(TB):
                v0_ip(FIRST, t)
            run_batches(act, batch)
            act.wait_ge(y_out, 16 * CBN * BATCH + 16)

        @block.vector
        def _(dve):
            for i, s in enumerate((freed["D"], max_half, max_chunk, z_done, zb_done, o_moved, low_block[0], low_block[1])):
                nc.vector.memset(stat[:, i, 0:1], 0.0).then_inc(s, CREDIT)
            nc.vector.memset(stat[:, 9, 0:1], 0.0).then_inc(y_out, 16)
            zero = [t[:, :] for t in q_slot + k_slot] + [t[:, :, :] for t in row_max[0] + row_max[1] + v0_slot]
            for t in zero:
                nc.vector.memset(t.bitcast(F32), 0.0)
            nc.vector.memset(v0_sb[:, :, :, :], 0.0)
            nc.vector.memset(ip_rows[:, :], 1.0)
            nc.vector.memset(dump[:, 8:9], 0.0).then_inc(chain, 1)
            dve.wait_ge(chain, 1)
            for slot in k_slot:
                nc.vector.memset(slot[SHIFT_ROW:SHIFT_ROW + 1, 0:TEXT0].bitcast(F32), -1.0)
                nc.vector.memset(slot[ALL_ROWS - 1:ALL_ROWS, TEXT0:T].bitcast(F32), -1.0)
            nc.vector.memset(ip_rows[0:TEXT0, :], 0.0)
            for slot in v0_slot:
                nc.vector.memset(slot[0:TEXT0, 0, D:D + 1].bitcast(F32), 1.0)
                nc.vector.memset(slot[:, :, 2 * D + 1:V0W].bitcast(F32), 1.0)
            nc.vector.memset(dump[:, 9:10], 0.0).then_inc(chain, 1)
            dve.wait_ge(chain, 2)
            for slot in v0_slot:
                last = nc.vector.memset(slot[0:TEXT0, 0, 2 * D + 1:V0W].bitcast(F32), 0.0)
            last.then_inc(dve_consts_in, 1)
            CHAIN0 = 2
            links = [0]
            CHAIN_B = 26

            def link(b, ins):
                links[0] += 1
                ins.then_inc(chain, 1)
                dve.wait_ge(chain, CHAIN_B * b + links[0] + CHAIN0)

            def low(b, name, m):
                wait_job(dve, b, name, m)
                k = HIGHS.index(name) * CBN + m
                dve.wait_ge(high_in, k - 2 * CBN + 1 if b is FIRST else 4 * CBN * b + 2 * CBN + k + 1)
                nc.vector.tensor_tensor(parts[name][1][0:CB[m], m, :], bank(name, m)[0:CB[m], :],
                                        parts[name][0][0:CB[m], m, :].bitcast(F32), ALU.subtract).then_inc(freed["D"], 1)

            def lowT(b, l, n, par, t):
                dve.wait_ge(pt_block[l], TB * (HEADS * b + n + 1) + t + 1 + CREDIT1)
                nc.vector.tensor_tensor(probsT_low[1 - par][:, t, :], probsT[:, t, :], probsT_high[1 - par][:, t, :].bitcast(F32),
                                        ALU.subtract).then_inc(low_block[l], 1)

            def step0(b, n, k, turn, use, transposed, scores):
                par = k % 2

                def maxima(half):
                    cs = slice(2 * half, 2 * half + 2)
                    dve.wait_ge(s_half, 2 * (HEADS * b + n + 2) + half + 1)
                    nc.vector.tensor_reduce(out=row_max[0][par][:, cs, 0:1], in_=ps_s[:, :, 0:TEXT0], axis=AX.X, op=ALU.max)
                    nc.vector.tensor_reduce(out=row_max[0][par][:, cs, SHIFT_ROWS - 1:SHIFT_ROWS], in_=ps_s[:, :, TEXT0:T],
                                            axis=AX.X, op=ALU.max).then_inc(max_half, 1)

                if scores:
                    maxima(0)
                if transposed:
                    lowT(b, 0, n, par, 0)
                if scores:
                    maxima(1)
                if transposed:
                    lowT(b, 0, n, par, 1)
                if use:
                    dve.wait_ge(o_done, HEADS * b + n + 1)
                    nc.vector.tensor_reduce(out=o0_all[:, n, :, :],
                                            in_=ps_b[:, 0:SC * V0S].rearrange("p (c a w) -> p c w a", c=SC, a=2),
                                            axis=AX.X, op=ALU.add).then_inc(o_moved, 1)
                if transposed:
                    lowT(b, 0, n, par, 2)

            def step1(b, n, k, turn, use, transposed, scores):
                par = k % 2
                g = HEADS * b + n

                def maxima(c):
                    if c == 0:
                        dve.wait_ge(sz_moved, g + 1) if use else None
                    dve.wait_ge(s_chunk, SC * (g + 2) + c + 1)
                    nc.vector.tensor_copy(sz[par][:, c, 0:IPN], ps_s[:, c % 2, TEXT1:T])
                    nc.vector.tensor_reduce(out=row_max[1][par][:, c, 0:1], in_=ps_s[:, c % 2, 0:TEXT1], axis=AX.X,
                                            op=ALU.max).then_inc(max_chunk, 1)

                out = head_out[par]
                if use:
                    dve.wait_ge(b_done, g + 1)
                    dve.wait_ge(p_chunk, SC * (g + 1) + CREDIT)
                    dve.wait_ge(out_moved, g - 1 + CREDIT)
                    for c in range(SC):
                        last = nc.vector.tensor_tensor_reduce(out=probs[par][:, c, 0:P], in0=ps_b[:, P * c:P * c + P],
                                                              in1=probs[par][:, c, 0:P], scale=1.0, scalar=0.0,
                                                              op0=ALU.mult, op1=ALU.add, accum_out=out[:, c, HO + 1:HO + 2])
                    last.then_inc(zb_done, 1)
                def products_used(c):
                    dve.wait_ge(w_done, SC * g + c + 1)
                    nc.vector.tensor_copy(out[:, c, 0:HO], ps_w[c % 2][:, GN:GW])
                    nc.vector.tensor_tensor_reduce(out=probs[par][:, c, P:TEXT1], in0=ps_w[c % 2][:, 0:GN],
                                                   in1=probs[par][:, c, P:TEXT1], scale=1.0, scalar=0.0,
                                                   op0=ALU.mult, op1=ALU.add, accum_out=out[:, c, HO:HO + 1]).then_inc(z_done, 1)

                for c in range(SC):
                    if use and c < 3:
                        products_used(c)
                    if scores:
                        maxima(c)
                    if not use and not transposed and c == 1:
                        ip_context(b)
                    if not use and transposed and c < 2:
                        ip_values(b, 2 * c)
                        ip_values(b, 2 * c + 1)
                    if use and c == 3:
                        products_used(c)
                    if transposed:
                        lowT(b, 1, n, par, c)

            def ip_context(b):
                wait_job(dve, b, "ipn", 0)
                nc.vector.tensor_copy(ip_norm2[:, :], bank("ipn", 0)[:, 0:IPN]).then_inc(freed["D"], 1)
                wait_job(dve, b, "vip", 0)
                nc.vector.tensor_copy(vip[:, :], bank("vip", 0)[0:IPN, 0:C]).then_inc(freed["D"], 1)

            def ip_values(b, i):
                wait_job(dve, b, "vrep", i)
                nc.vector.tensor_copy(vip_rep[:, i, :], bank("vrep", i)[:, 0:C]).then_inc(freed["D"], 1)

            def lows(b, name):
                for m in range(CBN):
                    low(b, name, m)

            def batch(b, ahead):
                links[0] = 0
                run_heads(step0, dve, b)
                dve.wait_ge(o_moved, HEADS * (b + 1) + CREDIT)
                o0 = out_all[:, :].rearrange("p (n w) -> p n w", w=V0W)
                zr = stat[:, :, 0:2]
                link(b, nc.vector.reciprocal(zr, o0.rearrange("p n (a w) -> p n a w", a=2)[:, :, :, D]))
                nc.vector.tensor_tensor(wide[0], o0[:, :, 0:D], stat[:, :, 0:1].to_broadcast([P, nd, D]), ALU.mult)
                link(b, nc.vector.tensor_tensor(wide[1], o0[:, :, D + 1:2 * D + 1], stat[:, :, 1:2].to_broadcast([P, nd, D]), ALU.mult))
                by_head = heads_out[:, :, :].rearrange("p c (h d) -> p h c d", d=D)
                w4 = [w.rearrange("p (h c) d -> p h c d", c=SC) for w in wide]
                nc.vector.tensor_tensor(by_head, w4[0], w4[1], ALU.add).then_inc(heads_ready, 1)
                lows(b, "k1")
                dve.wait_ge(ctx_in, 16 * b + 16)
                nc.vector.tensor_tensor(ip_sq[:, :, :], ctx_sb[:, :, TEXT1:T], ctx_sb[:, :, TEXT1:T], ALU.mult)\
                    .then_inc(ip_sq_in, 1)
                dve.wait_ge(y_out, 16 * CBN * b + 16)
                for m in range(CBN):
                    wait_job(dve, b, "x1", m)
                    nc.vector.scalar_tensor_tensor(out=x1_sb[0:CB[m], m, :], in0=bank("x1", m)[0:CB[m], :],
                                                   scalar=bias_o[0][0:CB[m], m:m + 1], in1=x_sb[0:CB[m], m, :],
                                                   op0=ALU.add, op1=ALU.add).then_inc(freed["D"], 1)
                lows(b, "q1")
                for i in range(TB):
                    wait_job(dve, b, "g", i)
                    dve.wait_ge(gram_high, TB * b + i + 1)
                    src = bank("g", i)
                    diag = P if i < TB - 1 else P - IPN
                    if i > 0:
                        cols = slice(P * (i - 1), P * (i - 1) + diag)
                        nc.vector.tensor_tensor(gram_low[:, i, cols], src[:, 0:diag], gram[0][:, i, cols].bitcast(F32), ALU.subtract)
                    cols = slice(P * i - P + diag, GA)
                    nc.vector.scalar_tensor_tensor(out=gram_low[:, i, cols], in0=src[:, diag:T - P * i], scalar=2.0,
                                                   in1=gram[0][:, i, cols].bitcast(F32), op0=ALU.mult, op1=ALU.subtract)\
                        .then_inc(freed["D"], 1)

                run_heads(step1, dve, b)
                dve.wait_ge(out_moved, HEADS * (b + 1) + CREDIT)
                dve.wait_ge(sz_moved, HEADS * (b + 1))
                o1 = out_all[:, 0:nd * OUT1].rearrange("p (n w) -> p n w", w=OUT1)
                szf = sz_all[:, :, :, :].rearrange("p h c w -> p (h c) w")
                rz, n2, rn = stat[:, :, 2:3], stat[:, :, 3:4], stat[:, :, 4:5]
                top, tot = stat[:, :, 5:6], stat[:, :, 6:7]
                link(b, nc.vector.reciprocal(rz, szf[:, :, IPN:IPN + 1]))
                link(b, nc.vector.tensor_tensor(n2, o1[:, :, NA:NA + 1], o1[:, :, NB:NB + 1], ALU.add))
                link(b, nc.vector.tensor_tensor(n2, n2, rz, ALU.mult))
                link(b, nc.vector.tensor_tensor(n2, n2, rz, ALU.mult))
                nc.vector.tensor_scalar_max(root[:, 0:nd], stat[:, :, 3], EPS * EPS)
                nc.vector.tensor_scalar_max(root[:, nd:nd + IPN], ip_norm2[:, :], EPS * EPS).then_inc(ask_root, 1)
                if ahead:
                    low(b, "k0", 0)
                dve.wait_ge(root_in, b + 1)
                nc.vector.reciprocal(rip[:, :], root[:, nd:nd + IPN])
                link(b, nc.vector.reciprocal(stat[:, :, 4], root[:, 0:nd]))
                link(b, nc.vector.tensor_tensor(rn, rn, rz, ALU.mult))
                link(b, nc.vector.tensor_tensor(fused[:, :, :], o1[:, :, A1:A1 + IPN], rn.to_broadcast([P, nd, IPN]), ALU.mult))
                for i in range(IPN):
                    last = nc.vector.tensor_scalar(fused[:, :, i], fused[:, :, i], rip[:, i:i + 1], SEM_SCALE / 2, ALU.mult, ALU.mult)
                link(b, last)
                link(b, nc.vector.scalar_tensor_tensor(out=fused[:, :, :], in0=szf[:, :, 0:IPN], scalar=SCALE, in1=fused[:, :, :],
                                                       op0=ALU.mult, op1=ALU.add))
                link(b, nc.vector.tensor_reduce(out=top, in_=fused[:, :, :], axis=AX.X, op=ALU.max))
                nc.vector.tensor_tensor(fused[:, :, :], fused[:, :, :], top.to_broadcast([P, nd, IPN]), ALU.subtract)\
                    .then_inc(ask_exp, 1)
                nc.vector.tensor_tensor(wide[0], o1[:, :, V1:V1 + D], rz.to_broadcast([P, nd, D]), ALU.mult)
                if ahead:
                    low(b, "k0", 1)
                    low(b, "k0", 2)
                dve.wait_ge(exp_in, b + 1)
                link(b, nc.vector.tensor_reduce(out=tot, in_=fused[:, :, :], axis=AX.X, op=ALU.add))
                link(b, nc.vector.reciprocal(tot, tot))
                tot3 = stat[:, :, 6].rearrange("p (h c) -> p h c", c=SC)
                mask3 = mask_sb[:, :].unsqueeze(1).to_broadcast([P, HEADS, SC])
                link(b, nc.vector.tensor_tensor(tot3, tot3, mask3, ALU.mult))
                link(b, nc.vector.tensor_tensor(fused[:, :, :], fused[:, :, :], tot.to_broadcast([P, nd, IPN]), ALU.mult))
                f4 = fused[:, :, :].rearrange("p (h c) i -> p h c i", c=SC)
                vr = vip_rep[:, :, :].rearrange("p i (h d) -> p i h d", d=D)
                for i in range(IPN):
                    for c in range(SC):
                        last = nc.vector.tensor_tensor(w4[1][:, :, c, :], f4[:, :, c, i:i + 1].to_broadcast([P, HEADS, D]),
                                                       vr[:, i, :, :], ALU.mult)
                    if ahead and i < 2:
                        for m in ((0,), (1, 2))[i]:
                            low(b, "q0", m)
                    link(b, last)
                    if i < IPN - 1:
                        link(b, nc.vector.tensor_tensor(wide[0], wide[0], wide[1], ALU.add))
                nc.vector.tensor_tensor(by_head, w4[0], w4[1], ALU.add).then_inc(heads_ready, 1)
                for m in range(CBN):
                    wait_job(dve, b, "y", m)
                    nc.vector.scalar_tensor_tensor(out=x1_sb[0:CB[m], m, :], in0=bank("y", m)[0:CB[m], :],
                                                   scalar=bias_o[1][0:CB[m], m:m + 1], in1=x1_sb[0:CB[m], m, :],
                                                   op0=ALU.add, op1=ALU.add).then_inc(freed["D"], 1)
                assert links[0] <= CHAIN_B, links[0]
                while links[0] < CHAIN_B:
                    link(b, nc.vector.memset(dump[:, 8:9], 0.0))

            lows(FIRST, "k0")
            lows(FIRST, "q0")
            run_batches(dve, batch)

        @block.tensor
        def _(pe):
            pe.wait_ge(built, 1)
            pe.wait_ge(ident_r_in, 1)
            pe.wait_ge(dve_consts_in, 1)

            def mm(out, lhsT, rhs, start, stop):
                return nc.tensor.matmul(out, lhsT, rhs, start=start, stop=stop)

            def free_bank(b, name, m):
                k = JOB[name, m]
                if b is not FIRST and k < RING:
                    for e in "AD":
                        pe.wait_ge(freed[e], freed_value(b, e, 0))
                elif k - RING >= FIRST_NEXT if b is FIRST else not left_out(b, k) or k - RING >= FIRST_NEXT + len(NEXT):
                    wait_freed(pe, b, *JOBS[k - RING][0:2])
                return bank(name, m)

            def over_e(out, lhs, rhs):
                for e in range(EB):
                    last = mm(out, lhs(e), rhs(e), e == 0, e == EB - 1)
                return last

            def over_c(out, w, m, src):
                for e in range(CBN):
                    last = mm(out, w[0:CB[e], e, m * P:m * P + CB[m]], src[0:CB[e], e, :], e == 0, e == CBN - 1)
                return last

            def scores_chunk(slot, c, out):
                return mm(out, q_slot[slot][0:SCORE_ROWS, P * c:P * c + P], k_slot[slot][0:SCORE_ROWS, :], True, True)

            def scoresT_block(slot, t, out):
                return mm(out, k_slot[slot][:, P * t:P * t + P], q_slot[slot][:, :], True, True)

            def scoresT_of(l, g, k, t):
                if t == 0:
                    pe.wait_ge(shift_in[l], g + 2)
                pe.wait_ge(pt_block[l], TB * (g + 1) + t - 1 + CREDIT1)
                scoresT_block((k + 1) % SLOTS, t, ps_t[:, t % 2, :]).then_inc(st_block[l], 1)

            def wait_slot(b, l, n, k, turn):
                pe.wait_ge(slots_in[l][(k + 2) % SLOTS], SLOT_LOADS * (TURNS * b + turn + (k + 2) // SLOTS + 1))

            def head_maxT(l, par):
                for c in range(SC):
                    rows = row_max[l][par][:, c, :]
                    last = mm(ps_m[0:SHIFT_ROWS, P * c:P * c + P], rows if l == 0 else rows.to_broadcast([P, SHIFT_ROWS]),
                              ident_r[:, :], True, True)
                last.then_inc(maxT_done[l], 1)

            def step0(b, n, k, turn, use, transposed, scores):
                par = k % 2
                g = HEADS * b + n

                def scores_half(half):
                    if half == 0:
                        wait_slot(b, 0, n, k, turn)
                    pe.wait_ge(max_half, 2 * (g + 2) + half + CREDIT)
                    for i in range(2):
                        last = scores_chunk((k + 2) % SLOTS, 2 * half + i, ps_s[:, i, :])
                    last.then_inc(s_half, 1)

                def values_high(t):
                    pe.wait_ge(pt_block[0], TB * g + t + 1 + CREDIT1)
                    mm(ps_w[par][0:V0S, :], v0_slot[par][:, t, :], probsT_high[par][:, t, :], t == 0, False)

                def values_low(t):
                    if t < TB - 1:
                        pe.wait_ge(low_block[0], (TB - 1) * g + t + 1 + CREDIT)
                    else:
                        pe.wait_ge(low_last, g + 1 + CREDIT)
                    return mm(ps_w[par][0:V0S, :], v0_slot[par][:, t, :], probsT_low[par][:, t, :], False, t == TB - 1)

                if scores:
                    scores_half(0)
                if use:
                    pe.wait_ge(oT_moved, g - 1 + CREDIT)
                    pe.wait_ge(v0_in, g + 1)
                    values_high(0)
                    values_high(1)
                    values_high(2)
                if transposed:
                    scoresT_of(0, g, k, 0)
                if use:
                    values_high(3)
                if transposed:
                    scoresT_of(0, g, k, 1)
                if use:
                    values_low(0)
                    values_low(1)
                    values_low(2)
                if scores:
                    scores_half(1)
                if use:
                    values_low(3).then_inc(oT_done, 1)
                if transposed:
                    scoresT_of(0, g, k, 2)
                    scoresT_of(0, g, k, 3)
                if scores:
                    pe.wait_ge(max_half, 2 * (g + 3) + CREDIT)
                    head_maxT(0, par)
                if use:
                    pe.wait_ge(oT_moved, g + 1 + CREDIT)
                    pe.wait_ge(o_moved, g + CREDIT)
                    pe.sem_inc(passed, 1)
                    for c in range(SC):
                        last = nc.tensor.transpose(ps_b[:, V0S * c:V0S * c + V0S], outT0[par][:, P * c:P * c + P],
                                                   ident[0:V0S, 0:V0S])
                    last.then_inc(o_done, 1)

            def step1(b, n, k, turn, use, transposed, scores):
                par = k % 2
                g = HEADS * b + n

                key_rows = [P] * (TB - 1) + [P - IPN]

                def gram_product(c):
                    pe.wait_ge(z_done, SC * g + c - 1 + CREDIT)
                    out, cols = ps_w[c % 2], slice(P * c, P * c + P)
                    for t in range(TB):
                        rows, lo = key_rows[t], P * max(t, 1) - P
                        high = probsT_high[par][0:rows, t, cols]
                        mm(out[:, lo:GW], high, gram[par][0:rows, t, lo:GW], t == 0, False)
                        mm(out[:, lo:GA], high, gram_low[0:rows, t, lo:GA], False, False)
                    for t in range(TB):
                        rows, lo = key_rows[t], P * max(t, 1) - P
                        if c == 0:
                            pe.wait_ge(low_block[1], TB * g + t + 1 + CREDIT)
                        last = mm(out[:, lo:GV], probsT_low[par][0:rows, t, cols], gram[par][0:rows, t, lo:GV], False, t == TB - 1)
                    last.then_inc(w_done, 1)

                def scores_of(c):
                    if c == 0:
                        wait_slot(b, 1, n, k, turn)
                    pe.wait_ge(p_chunk, SC * (g + 2) + c - 1 + CREDIT)
                    scores_chunk((k + 2) % SLOTS, c, ps_s[:, c % 2, :]).then_inc(s_chunk, 1)

                if use:
                    pe.wait_ge(pt_block[1], TB * g + 1 + CREDIT1)
                    pe.wait_ge(zb_done, g + CREDIT)
                    for c in range(SC):
                        last = mm(ps_b[:, P * c:P * c + P], probsT[:, 0, P * c:P * c + P], gram00[:, :], True, True)
                    last.then_inc(b_done, 1)
                if transposed:
                    pe.wait_ge(max_chunk, SC * (g + 2) + CREDIT)
                    head_maxT(1, 1 - par)
                if use:
                    pe.wait_ge(pt_block[1], TB * (g + 1) + CREDIT1)
                    pe.wait_ge(v_in, g + 1)
                    gram_product(0)
                if transposed:
                    scoresT_of(1, g, k, 0)
                if scores:
                    scores_of(0)
                if not use and transposed:
                    ip_values(b, 0)
                    ip_values(b, 1)
                if use:
                    gram_product(1)
                if transposed:
                    scoresT_of(1, g, k, 1)
                if scores:
                    scores_of(1)
                if not use and not transposed:
                    ip_context(b)
                if not use and transposed:
                    ip_values(b, 2)
                    ip_values(b, 3)
                if use:
                    gram_product(2)
                if transposed:
                    scoresT_of(1, g, k, 2)
                if scores:
                    scores_of(2)
                if transposed:
                    scoresT_of(1, g, k, 3)
                if scores:
                    scores_of(3)
                if use:
                    gram_product(3)

            def ip_context(b):
                pe.wait_ge(ip_sq_in, b + 1)
                over_e(bank("ipn", 0)[:, 0:IPN], lambda e: ones[:, :].to_broadcast([P, P]), lambda e: ip_sq[:, e, :]).then_inc(job_done, 1)
                over_e(bank("vip", 0)[0:IPN, 0:C], lambda e: ctx_sb[:, e, TEXT1:T], lambda e: w_big["vi1"][:, e, :])\
                    .then_inc(job_done, 1)

            def ip_values(b, i):
                wait_freed(pe, b, *(("vip", 0) if i < 2 else ("vrep", i - 2)))
                mm(bank("vrep", i)[:, 0:C], ident[0:IPN, i:i + 1].to_broadcast([IPN, P]), vip[:, :], True, True).then_inc(job_done, 1)

            def keys(b, name, split, text):
                for m in range(CBN):
                    out, cols = free_bank(b, name, m), slice(m * P, m * P + CB[m])
                    over_e(out[0:CB[m], 0:text], lambda e: w_big[name][:, e, cols], lambda e: ctx_sb[:, e, 0:text])
                    over_e(out[0:CB[m], text:T], lambda e: w_big[split][:, e, cols], lambda e: ctx_sb[:, e, text:T])\
                        .then_inc(job_done, 1)

            def by_channels(b, name, w, src):
                for m in range(CBN):
                    over_c(free_bank(b, name, m)[0:CB[m], :], w_small[w], m, src).then_inc(job_done, 1)

            def by_keys(b, name, w):
                for t in range(TB):
                    over_e(free_bank(b, name, t)[:, 0:C], lambda e: ctx_sb[:, e, P * t:P * t + P],
                           lambda e: w_big[w][:, e, :]).then_inc(job_done, 1)

            def for_layer0(b, batch):
                pe.wait_ge(ctx_in, 16 * batch + 16)
                if b is FIRST:
                    pe.wait_ge(weights0_in["k"], 32)
                keys(b, "k0", "ki0", TEXT0)
                pe.wait_ge(x_in, 32 * batch + 32)
                if b is FIRST:
                    pe.wait_ge(weights0_in["q"], 32)
                by_channels(b, "q0", "q0", x_sb)
                if b is FIRST:
                    pe.wait_ge(weights0_in["v"], 32)
                over_e(free_bank(b, "v0t", 0)[0:TEXT0, 0:C], lambda e: ctx_sb[:, e, 0:TEXT0],
                       lambda e: w_big["v0"][:, e, :]).then_inc(job_done, 1)
                by_keys(b, "v0i", "vi0")

            def transposed_heads(b, name, l):
                pe.wait_ge(heads_ready, 2 * b + l + 1)
                for m in range(CBN):
                    out = free_bank(b, name, m)
                    pe.sem_inc(passed, 1)
                    for c in range(SC):
                        last = nc.tensor.transpose(out[0:CB[m], P * c:P * c + P], heads_out[:, c, P * m:P * m + CB[m]],
                                                   ident[:, :])
                    last.then_inc(job_done, 1)
                wait_freed(pe, b, name, CBN - 1)

            def batch(b, ahead):
                run_heads(step0, pe, b)
                keys(b, "k1", "ki1", TEXT1)
                transposed_heads(b, "tr0", 0)
                by_channels(b, "x1", "o0", heads_outT)
                wait_freed(pe, b, "x1", CBN - 1)
                by_channels(b, "q1", "q1", x1_sb)
                for i in range(TB):
                    over_e(free_bank(b, "g", i)[:, 0:T - P * i], lambda e: ctx_sb[:, e, P * i:P * i + P],
                           lambda e: ctx_sb[:, e, P * i:T]).then_inc(job_done, 1)
                by_keys(b, "v1", "v1")
                wait_freed(pe, b, "v1", TB - 1)

                def before_use():
                    wait_freed(pe, b, "vrep", IPN - 1)
                    pe.wait_ge(gram_copied, b + 1)
                    pe.sem_inc(passed, 1)

                run_heads(step1, pe, b, before_use)
                if ahead:
                    for_layer0(b, b + 1)
                transposed_heads(b, "tr1", 1)
                by_channels(b, "y", "o1", heads_outT)
                if ahead:
                    wait_freed(pe, b, "y", CBN - 1)

            for_layer0(FIRST, 0)
            wait_freed(pe, FIRST, "v0i", TB - 1)
            wait_freed(pe, FIRST, "q0", CBN - 1)
            pe.wait_ge(weights_in, WEIGHTS)
            run_batches(pe, batch)


def kernel(x, ctx_2048, fside_S_0, L0_xattn_Wq, L0_xattn_Wk, L0_xattn_Wv, L0_xattn_Wk_ip, L0_xattn_Wv_ip, L0_xattn_Wo,
           L0_xattn_bo, L1_xattn_W_q, L1_xattn_W_k, L1_xattn_W_v, L1_xattn_W_k_ip, L1_xattn_W_v_ip, L1_xattn_W_out,
           L1_xattn_b_out):
    import numpy as np
    import concourse.bacc as bacc
    from concourse.bass_utils import run_bass_kernel_spmd

    given = {
        "xT": np.asarray(x).transpose(0, 2, 1),
        "ctxT": np.asarray(ctx_2048).transpose(0, 2, 1),
        "mask": np.asarray(fside_S_0).reshape(SC, P).T,
        "wq0": np.asarray(L0_xattn_Wq).T,
        "wk0": np.asarray(L0_xattn_Wk).T,
        "wv0": np.asarray(L0_xattn_Wv).T,
        "wki0": np.asarray(L0_xattn_Wk_ip).T,
        "wvi0": np.asarray(L0_xattn_Wv_ip).T,
        "wo0": np.asarray(L0_xattn_Wo).T,
        "bo0": np.asarray(L0_xattn_bo).reshape(C, 1),
        "wq1": np.asarray(L1_xattn_W_q),
        "wk1": np.asarray(L1_xattn_W_k),
        "wv1": np.asarray(L1_xattn_W_v),
        "wki1": np.asarray(L1_xattn_W_k_ip),
        "wvi1": np.asarray(L1_xattn_W_v_ip),
        "wo1": np.asarray(L1_xattn_W_out),
        "bo1": np.asarray(L1_xattn_b_out).reshape(C, 1),
    }
    nc = bacc.Bacc("TRN2", target_bir_lowering=False, num_devices=1)
    arrays, args = {}, []
    for name, a in given.items():
        a = np.ascontiguousarray(a)
        arrays[f"in_{name}"] = a
        args.append(nc.dram_tensor(f"in_{name}", a.shape, mybir.dt.from_np(a.dtype), kind="ExternalInput").ap())
    out = nc.dram_tensor("outT", [BATCH, C, S], F32, kind="ExternalOutput").ap()
    build(nc, *args, out)
    r = run_bass_kernel_spmd(nc, [arrays], core_ids=[0])
    return np.ascontiguousarray(r.results[0]["outT"].transpose(0, 2, 1))
```
